# Optimizing a Trainium2 kernel written in Bass

```python
import numpy as np
import jax
import jax.numpy as jnp

def _softmax(x, axis=-1):
    return jax.nn.softmax(x, axis=axis)

def _gelu(x):
    return jax.nn.gelu(x, approximate=True)

def _silu(x):
    return jax.nn.silu(x)

def _sigmoid(x):
    return jax.nn.sigmoid(x)

def _layernorm(x, axis=-1, eps=1e-05):
    m = jnp.mean(x, axis=axis, keepdims=True)
    v = jnp.var(x, axis=axis, keepdims=True)
    return (x - m) / jnp.sqrt(v + eps)

def _scatter_add(tgt, idx, src, axis=0):
    return tgt.at[idx].add(src)

def _segment_sum(src, seg, n):
    return jax.ops.segment_sum(src, seg, n)
kernel_name = 'mk_xattn_seq_d2_seqx_r4_c02733'

def setup_inputs(seed: int=0):
    np.random.seed(seed)
    _w = jnp.asarray

    def _rec_inputs():
        import jax
        import jax.numpy as jnp
        _rk = jax.random.key(seed)
        x = -0.0002928 + 1 * jax.random.normal(jax.random.fold_in(_rk, 1), (16, 128, 512), jnp.float32)
        _lenS = 128 - jax.random.randint(jax.random.fold_in(_rk, 7), (16,), 0, max(1, 128 // 4) + 1, jnp.int32)
        _lenS2 = 128 - jax.random.randint(jax.random.fold_in(_rk, 8), (16,), 0, max(1, 128 // 4) + 1, jnp.int32)
        _ctx_2048P = jax.random.normal(jax.random.fold_in(_rk, 11), (16, 16, 512), jnp.float32)
        _ctx_2048c = jax.random.dirichlet(jax.random.fold_in(_rk, 511), 0.3 * jnp.ones((16,), jnp.float32), (16, 128))
        _ctx_2048t = jnp.einsum('bsk,bkd->bsd', _ctx_2048c, _ctx_2048P)
        _ctx_2048t = _ctx_2048t * jax.lax.rsqrt(jnp.mean(jnp.square(_ctx_2048t)) + 1e-12) * 0.953939
        ctx_2048 = -1.39393e-06 + 0.999914 * (_ctx_2048t + 0.3 * jax.random.normal(jax.random.fold_in(_rk, 611), (16, 128, 512), jnp.float32))
        _validS = jnp.arange(128)[None, :] < _lenS[:, None]
        _validS2 = jnp.arange(128)[None, :] < _lenS2[:, None]
        _causal = jnp.tril(jnp.ones((128, 128), dtype=bool))
        mask_1x1xSxS2_fc1 = jnp.where(jnp.broadcast_to(_validS2[0:1, None, None, :], (1, 1, 128, 128)), 1.0, 0.0).astype(jnp.float32)
        mask_Bx1xSxS2_ff1 = jnp.where(jnp.ones((16, 1, 128, 128), dtype=bool), 1.0, 0.0).astype(jnp.float32)
        mask_Bx1xSxS2_ff0 = jnp.where(jnp.ones((16, 1, 128, 128), dtype=bool), 0.0, -1000000000.0).astype(jnp.float32)
        return (x, ctx_2048, mask_1x1xSxS2_fc1, mask_Bx1xSxS2_ff1, mask_Bx1xSxS2_ff0)
    x, ctx_2048, mask_1x1xSxS2_fc1, mask_Bx1xSxS2_ff1, mask_Bx1xSxS2_ff0 = _rec_inputs()

    def _L0_xattn_setup():
        import jax, jax.numpy as jnp
        import numpy as np
        H = 512
        NH = 16
        HD = H // NH
        EPS = 1e-05

        def gelu(x):
            return 0.5 * x * (1.0 + jnp.tanh(0.7978845608028654 * x * (1.0 + 0.044715 * x * x)))

        def layernorm(x, scale, bias):
            m = jnp.mean(x, axis=-1, keepdims=True)
            v = jnp.mean(jnp.square(x - m), axis=-1, keepdims=True)
            return (x - m) * jax.lax.rsqrt(v + EPS) * scale + bias

        def split_heads(x):
            b, s, _ = x.shape
            return x.reshape(b, s, NH, HD).transpose(0, 2, 1, 3)

        def merge_heads(x):
            b, nh, s, hd = x.shape
            return x.transpose(0, 2, 1, 3).reshape(b, s, nh * hd)

        def attention(q, k, v, mask):
            scores = jnp.einsum('bhqd,bhkd->bhqk', q, k) / jnp.sqrt(jnp.float32(HD))
            scores = scores * mask - 10000.0 * (1.0 - mask)
            probs = jax.nn.softmax(scores, axis=-1)
            return jnp.einsum('bhqk,bhkd->bhqd', probs, v)
        key = jax.random.key(seed)
        ks = jax.random.split(key, 16)
        b, s, t = (2, 256, 256)
        w = lambda k, i, o: jax.random.normal(k, (i, o), jnp.float32) * 0.02
        inp = {'hidden_states': jax.random.normal(ks[0], (b, s, H), jnp.float32), 'encoder_states': jax.random.normal(ks[1], (b, t, H), jnp.float32), 'ltor_mask': jnp.tril(jnp.ones((1, 1, s, s), jnp.float32)), 'cross_mask': jnp.ones((b, 1, s, t), jnp.float32), 'ln1_s': jnp.ones((H,), jnp.float32), 'ln1_b': jnp.zeros((H,), jnp.float32), 'w_qkv': w(ks[2], H, 3 * H), 'b_qkv': jnp.zeros((3 * H,), jnp.float32), 'w_ao': w(ks[3], H, H), 'b_ao': jnp.zeros((H,), jnp.float32), 'ln2_s': jnp.ones((H,), jnp.float32), 'ln2_b': jnp.zeros((H,), jnp.float32), 'w_q': w(ks[4], H, H), 'b_q': jnp.zeros((H,), jnp.float32), 'w_kv': w(ks[5], H, 2 * H), 'b_kv': jnp.zeros((2 * H,), jnp.float32), 'w_co': w(ks[6], H, H), 'b_co': jnp.zeros((H,), jnp.float32), 'ln3_s': jnp.ones((H,), jnp.float32), 'ln3_b': jnp.zeros((H,), jnp.float32), 'w1': w(ks[7], H, 4 * H), 'b1': jnp.zeros((4 * H,), jnp.float32), 'w2': w(ks[8], 4 * H, H), 'b2': jnp.zeros((H,), jnp.float32)}
        return inp
    _L0_xattn_all = _L0_xattn_setup()
    _L0_xattn_in = {k: v for k, v in _L0_xattn_all.items() if k in ('ln1_s', 'ln1_b', 'w_qkv', 'b_qkv', 'w_ao', 'b_ao', 'ln2_s', 'ln2_b', 'w_q', 'b_q', 'w_kv', 'b_kv', 'w_co', 'b_co', 'ln3_s', 'ln3_b', 'w1', 'b1', 'w2', 'b2')}
    del _L0_xattn_all

    def _L1_xattn_setup():
        import jax, jax.numpy as jnp
        import numpy as np
        H = 512
        NH = 32
        KVH = 8
        HD = H // NH
        GROUPS = NH // KVH
        EPS = 1e-06
        B, L, S = (4, 256, 256)

        def _gqa_forward(hidden_state, encoder_hidden_state, encoder_attention_mask, Wq, bq, Wk, bk, Wv, bv, Wo, bo, gamma, beta):
            b, l, _ = hidden_state.shape
            s = encoder_hidden_state.shape[1]
            q = hidden_state @ Wq + bq
            k = encoder_hidden_state @ Wk + bk
            v = encoder_hidden_state @ Wv + bv
            q = q.reshape(b, l, KVH, GROUPS, HD).transpose(0, 2, 3, 1, 4)
            k = k.reshape(b, s, KVH, HD).transpose(0, 2, 1, 3)
            v = v.reshape(b, s, KVH, HD).transpose(0, 2, 1, 3)
            scale = 1.0 / jnp.sqrt(jnp.asarray(HD, q.dtype))
            scores = jnp.einsum('bkgld,bksd->bkgls', q, k) * scale
            scores = scores + encoder_attention_mask[:, :, None, :, :]
            attn = jax.nn.softmax(scores, axis=-1)
            out = jnp.einsum('bkgls,bksd->bkgld', attn, v)
            out = out.transpose(0, 3, 1, 2, 4).reshape(b, l, H)
            out = out @ Wo + bo
            x = out + hidden_state
            mu = jnp.mean(x, axis=-1, keepdims=True)
            var = jnp.var(x, axis=-1, keepdims=True)
            return (x - mu) * jax.lax.rsqrt(var + EPS) * gamma + beta
        key = jax.random.key(seed)
        ks = jax.random.split(key, 12)
        sd = 0.02
        return {'hidden_state': jax.random.normal(ks[0], (B, L, H), jnp.float32), 'encoder_hidden_state': jax.random.normal(ks[1], (B, S, H), jnp.float32), 'encoder_attention_mask': jnp.zeros((B, 1, L, S), jnp.float32), 'Wq': jax.random.normal(ks[2], (H, H), jnp.float32) * sd, 'bq': jnp.zeros((H,), jnp.float32), 'Wk': jax.random.normal(ks[3], (H, KVH * HD), jnp.float32) * sd, 'bk': jnp.zeros((KVH * HD,), jnp.float32), 'Wv': jax.random.normal(ks[4], (H, KVH * HD), jnp.float32) * sd, 'bv': jnp.zeros((KVH * HD,), jnp.float32), 'Wo': jax.random.normal(ks[5], (H, H), jnp.float32) * sd, 'bo': jnp.zeros((H,), jnp.float32), 'gamma': jnp.ones((H,), jnp.float32), 'beta': jnp.zeros((H,), jnp.float32)}
    _L1_xattn_all = _L1_xattn_setup()
    _L1_xattn_in = {k: v for k, v in _L1_xattn_all.items() if k in ('Wq', 'bq', 'Wk', 'bk', 'Wv', 'bv', 'Wo', 'bo', 'gamma', 'beta')}
    del _L1_xattn_all
    return {'x': x, 'ctx_2048': ctx_2048, 'mask_1x1xSxS2_fc1': mask_1x1xSxS2_fc1, 'mask_Bx1xSxS2_ff1': mask_Bx1xSxS2_ff1, 'mask_Bx1xSxS2_ff0': mask_Bx1xSxS2_ff0, 'L0_xattn_ln1_s': _L0_xattn_in['ln1_s'], 'L0_xattn_ln1_b': _L0_xattn_in['ln1_b'], 'L0_xattn_w_qkv': _L0_xattn_in['w_qkv'], 'L0_xattn_b_qkv': _L0_xattn_in['b_qkv'], 'L0_xattn_w_ao': _L0_xattn_in['w_ao'], 'L0_xattn_b_ao': _L0_xattn_in['b_ao'], 'L0_xattn_ln2_s': _L0_xattn_in['ln2_s'], 'L0_xattn_ln2_b': _L0_xattn_in['ln2_b'], 'L0_xattn_w_q': _L0_xattn_in['w_q'], 'L0_xattn_b_q': _L0_xattn_in['b_q'], 'L0_xattn_w_kv': _L0_xattn_in['w_kv'], 'L0_xattn_b_kv': _L0_xattn_in['b_kv'], 'L0_xattn_w_co': _L0_xattn_in['w_co'], 'L0_xattn_b_co': _L0_xattn_in['b_co'], 'L0_xattn_ln3_s': _L0_xattn_in['ln3_s'], 'L0_xattn_ln3_b': _L0_xattn_in['ln3_b'], 'L0_xattn_w1': _L0_xattn_in['w1'], 'L0_xattn_b1': _L0_xattn_in['b1'], 'L0_xattn_w2': _L0_xattn_in['w2'], 'L0_xattn_b2': _L0_xattn_in['b2'], 'L1_xattn_Wq': _L1_xattn_in['Wq'], 'L1_xattn_bq': _L1_xattn_in['bq'], 'L1_xattn_Wk': _L1_xattn_in['Wk'], 'L1_xattn_bk': _L1_xattn_in['bk'], 'L1_xattn_Wv': _L1_xattn_in['Wv'], 'L1_xattn_bv': _L1_xattn_in['bv'], 'L1_xattn_Wo': _L1_xattn_in['Wo'], 'L1_xattn_bo': _L1_xattn_in['bo'], 'L1_xattn_gamma': _L1_xattn_in['gamma'], 'L1_xattn_beta': _L1_xattn_in['beta']}

def reference(x, ctx_2048, mask_1x1xSxS2_fc1, mask_Bx1xSxS2_ff1, mask_Bx1xSxS2_ff0, L0_xattn_ln1_s, L0_xattn_ln1_b, L0_xattn_w_qkv, L0_xattn_b_qkv, L0_xattn_w_ao, L0_xattn_b_ao, L0_xattn_ln2_s, L0_xattn_ln2_b, L0_xattn_w_q, L0_xattn_b_q, L0_xattn_w_kv, L0_xattn_b_kv, L0_xattn_w_co, L0_xattn_b_co, L0_xattn_ln3_s, L0_xattn_ln3_b, L0_xattn_w1, L0_xattn_b1, L0_xattn_w2, L0_xattn_b2, L1_xattn_Wq, L1_xattn_bq, L1_xattn_Wk, L1_xattn_bk, L1_xattn_Wv, L1_xattn_bv, L1_xattn_Wo, L1_xattn_bo, L1_xattn_gamma, L1_xattn_beta):
    import jax
    import jax.numpy as jnp

    def _L0_xattn_ref(hidden_states, encoder_states, ltor_mask, cross_mask, ln1_s, ln1_b, w_qkv, b_qkv, w_ao, b_ao, ln2_s, ln2_b, w_q, b_q, w_kv, b_kv, w_co, b_co, ln3_s, ln3_b, w1, b1, w2, b2):
        import jax, jax.numpy as jnp
        import numpy as np
        H = 512
        NH = 16
        HD = H // NH
        EPS = 1e-05

        def gelu(x):
            return 0.5 * x * (1.0 + jnp.tanh(0.7978845608028654 * x * (1.0 + 0.044715 * x * x)))

        def layernorm(x, scale, bias):
            m = jnp.mean(x, axis=-1, keepdims=True)
            v = jnp.mean(jnp.square(x - m), axis=-1, keepdims=True)
            return (x - m) * jax.lax.rsqrt(v + EPS) * scale + bias

        def split_heads(x):
            b, s, _ = x.shape
            return x.reshape(b, s, NH, HD).transpose(0, 2, 1, 3)

        def merge_heads(x):
            b, nh, s, hd = x.shape
            return x.transpose(0, 2, 1, 3).reshape(b, s, nh * hd)

        def attention(q, k, v, mask):
            scores = jnp.einsum('bhqd,bhkd->bhqk', q, k) / jnp.sqrt(jnp.float32(HD))
            scores = scores * mask - 10000.0 * (1.0 - mask)
            probs = jax.nn.softmax(scores, axis=-1)
            return jnp.einsum('bhqk,bhkd->bhqd', probs, v)
        ln_out = layernorm(hidden_states, ln1_s, ln1_b)
        qkv = ln_out @ w_qkv + b_qkv
        q, k, v = jnp.split(qkv, 3, axis=-1)
        ctx = merge_heads(attention(split_heads(q), split_heads(k), split_heads(v), ltor_mask))
        attn_out = ctx @ w_ao + b_ao
        x = hidden_states + attn_out
        ln_out = layernorm(x, ln2_s, ln2_b)
        q = ln_out @ w_q + b_q
        kv = encoder_states @ w_kv + b_kv
        k, v = jnp.split(kv, 2, axis=-1)
        ctx = merge_heads(attention(split_heads(q), split_heads(k), split_heads(v), cross_mask))
        cross_out = ctx @ w_co + b_co
        x = x + cross_out
        ln_out = layernorm(x, ln3_s, ln3_b)
        mlp_out = gelu(ln_out @ w1 + b1) @ w2 + b2
        return x + mlp_out

    def _L1_xattn_ref(hidden_state, encoder_hidden_state, encoder_attention_mask, Wq, bq, Wk, bk, Wv, bv, Wo, bo, gamma, beta):
        import jax, jax.numpy as jnp
        import numpy as np
        H = 512
        NH = 32
        KVH = 8
        HD = H // NH
        GROUPS = NH // KVH
        EPS = 1e-06
        B, L, S = (4, 256, 256)

        def _gqa_forward(hidden_state, encoder_hidden_state, encoder_attention_mask, Wq, bq, Wk, bk, Wv, bv, Wo, bo, gamma, beta):
            b, l, _ = hidden_state.shape
            s = encoder_hidden_state.shape[1]
            q = hidden_state @ Wq + bq
            k = encoder_hidden_state @ Wk + bk
            v = encoder_hidden_state @ Wv + bv
            q = q.reshape(b, l, KVH, GROUPS, HD).transpose(0, 2, 3, 1, 4)
            k = k.reshape(b, s, KVH, HD).transpose(0, 2, 1, 3)
            v = v.reshape(b, s, KVH, HD).transpose(0, 2, 1, 3)
            scale = 1.0 / jnp.sqrt(jnp.asarray(HD, q.dtype))
            scores = jnp.einsum('bkgld,bksd->bkgls', q, k) * scale
            scores = scores + encoder_attention_mask[:, :, None, :, :]
            attn = jax.nn.softmax(scores, axis=-1)
            out = jnp.einsum('bkgls,bksd->bkgld', attn, v)
            out = out.transpose(0, 3, 1, 2, 4).reshape(b, l, H)
            out = out @ Wo + bo
            x = out + hidden_state
            mu = jnp.mean(x, axis=-1, keepdims=True)
            var = jnp.var(x, axis=-1, keepdims=True)
            return (x - mu) * jax.lax.rsqrt(var + EPS) * gamma + beta
        return _gqa_forward(hidden_state, encoder_hidden_state, encoder_attention_mask, Wq, bq, Wk, bk, Wv, bv, Wo, bo, gamma, beta)
    x = _L0_xattn_ref(x, ctx_2048, mask_1x1xSxS2_fc1, mask_Bx1xSxS2_ff1, L0_xattn_ln1_s, L0_xattn_ln1_b, L0_xattn_w_qkv, L0_xattn_b_qkv, L0_xattn_w_ao, L0_xattn_b_ao, L0_xattn_ln2_s, L0_xattn_ln2_b, L0_xattn_w_q, L0_xattn_b_q, L0_xattn_w_kv, L0_xattn_b_kv, L0_xattn_w_co, L0_xattn_b_co, L0_xattn_ln3_s, L0_xattn_ln3_b, L0_xattn_w1, L0_xattn_b1, L0_xattn_w2, L0_xattn_b2)
    x = _L1_xattn_ref(x, ctx_2048, mask_Bx1xSxS2_ff0, L1_xattn_Wq, L1_xattn_bq, L1_xattn_Wk, L1_xattn_bk, L1_xattn_Wv, L1_xattn_bv, L1_xattn_Wo, L1_xattn_bo, L1_xattn_gamma, L1_xattn_beta)
    return x

_drawn_inputs = setup_inputs


def setup_inputs(seed=0):
    import zlib

    import numpy as np

    out = dict(_drawn_inputs(seed))
    spreads = {'L0_xattn_ln1_s': (1.0, 0.6),
     'L0_xattn_ln1_b': (0.0, 0.4),
     'L0_xattn_b_qkv': (0.0, 0.1),
     'L0_xattn_b_ao': (0.0, 0.1),
     'L0_xattn_ln2_s': (1.0, 0.6),
     'L0_xattn_ln2_b': (0.0, 0.8),
     'L0_xattn_b_q': (0.0, 2.0),
     'L0_xattn_b_kv': (0.0, 0.1),
     'L0_xattn_b_co': (0.0, 0.1),
     'L0_xattn_ln3_s': (1.0, 0.2),
     'L0_xattn_ln3_b': (0.0, 0.327),
     'L0_xattn_b1': (0.0, 0.1),
     'L0_xattn_b2': (0.0, 0.1),
     'L1_xattn_bq': (0.0, 0.8),
     'L1_xattn_bk': (0.0, 2.0),
     'L1_xattn_bv': (0.0, 0.1),
     'L1_xattn_bo': (0.0, 0.1),
     'L1_xattn_gamma': (1.0, 0.2),
     'L1_xattn_beta': (0.0, 0.1)}
    factors = {'L0_xattn_w_q': 7.077, 'L1_xattn_Wq': 7.322, 'L1_xattn_Wk': 7.125}
    for name, (base, spread) in spreads.items():
        noise = np.random.default_rng([zlib.crc32(name.encode()), seed]).standard_normal(out[name].shape)
        drawn = base * np.exp(spread * noise) if base else spread * noise
        out[name] = jnp.asarray(drawn.astype(out[name].dtype))
    for name, factor in factors.items():
        out[name] = (out[name] * factor).astype(out[name].dtype)
    return out
```

```python
from contextlib import ExitStack

import concourse.bass as bass
from concourse import mybir

F32 = mybir.dt.float32
F32R = mybir.dt.float32r
ALU = mybir.AluOpType
ACT = mybir.ActivationFunctionType
AX = mybir.AxisListType

P = 128
QUAD = 32
GB = 4
TOK = GB * P
BANK = 512
UH = 8


AHEAD = 2


def nth(g, per, n):
    return g * per + (n + 1 + AHEAD)


def plain(g, per, n):
    return g * per + (n + 1)


class Semaphores:

    def __init__(self, nc, ctx):
        self.nc, self.ctx, self.by_name = nc, ctx, {}

    def named(self, name):
        if name not in self.by_name:
            self.by_name[name] = self.ctx.enter_context(self.nc.semaphore(name))
        return self.by_name[name]

    def clear(self):
        with self.nc.Block() as block:
            @block.sync
            def _(sp):
                for done in self.by_name.values():
                    sp.sem_clear(done)


class Shape:

    def __init__(self, x, w1):
        self.NB, self.S, self.D = x.shape
        self.C = self.D // P
        self.G = self.NB // GB
        self.F = w1.shape[1]
        self.M = self.F // P


def column(v):
    return v.rearrange("(c p) -> p c", p=P)


def weight(w):
    return w.rearrange("(k p) n -> p k n", p=P)


def three(high_a, low_a, high_b, low_b):
    return ((low_a, high_b), (high_a, low_b), (high_a, high_b))


def prepare_weights(nc, sems, name, units, stage_cols, rows=None):
    with ExitStack() as ctx:
        stage = ctx.enter_context(nc.sbuf_tensor(f"{name}_stage", [P, 3, 4, stage_cols], F32))
        loaded = [sems.named(f"loaded{i}") for i in range(3)]
        high_done = sems.named("high_done")
        low_done = sems.named("low_done")
        vectors_in = sems.named("vectors_in")
        values_spread = sems.named("values_spread")
        row_product = sems.named("row_product")
        row_done = sems.named("row_done")
        if rows is not None:
            value_columns, out_bias, row_tile = rows
            vcol = ctx.enter_context(nc.sbuf_tensor(f"{name}_vcol", [P, 4], F32))
            spread = ctx.enter_context(nc.sbuf_tensor(f"{name}_spread", [P, 4, P], F32))
            row_ps = ctx.enter_context(nc.psum_tensor(f"{name}_row_ps", [P, BANK], F32))
        block = ctx.enter_context(nc.Block())
        last = len(units) - 1

        @block.sync
        def _(sp):
            if rows is not None:
                for at, n, src in value_columns:
                    sp.dma_start(vcol[at:at + n, :], src, allow_slow_non_contiguous=True).then_inc(vectors_in, 16)
                sp.dma_start(row_tile[:, :], out_bias.partition_broadcast(P)).then_inc(vectors_in, 16)
            for i, (src, high, low) in enumerate(units):
                if i >= 3:
                    sp.wait_ge(high_done, i - 2)
                    sp.wait_ge(low_done, i - 2)
                k, n = src.shape[1], src.shape[2]
                sp.dma_start(stage[:, i % 3, 0:k, 0:n], src).then_inc(loaded[i % 3], 16)

        @block.scalar
        def _(act):
            for i, (src, high, low) in enumerate(units):
                k, n = src.shape[1], src.shape[2]
                act.wait_ge(loaded[i % 3], 16 * (i // 3 + 1))
                nc.scalar.copy(high, stage[:, i % 3, 0:k, 0:n]).then_inc(high_done, 1)

        @block.vector
        def _(dve):
            if rows is not None:
                dve.wait_ge(vectors_in, 16 * (len(value_columns) + 1))
                nc.vector.memset(spread[:, :, :], 1.0).then_inc(values_spread, 1)
                dve.wait_ge(values_spread, 1)
                for c in range(4):
                    nc.vector.tensor_scalar(spread[:, c, :], spread[:, c, :], vcol[:, c:c + 1], None,
                                            ALU.mult).then_inc(values_spread, 1)
            for i, (src, high, low) in enumerate(units):
                k, n = src.shape[1], src.shape[2]
                dve.wait_ge(high_done, i + 1)
                nc.vector.tensor_tensor(low, stage[:, i % 3, 0:k, 0:n], high.bitcast(F32),
                                        ALU.subtract).then_inc(low_done, 1)
            if rows is not None:
                dve.wait_ge(row_product, 1)
                nc.vector.tensor_tensor(rows[2][:, :], row_ps[:, :], rows[2][:, :],
                                        ALU.add).then_inc(row_done, 1)

        @block.tensor
        def _(pe):
            if rows is not None:
                pe.wait_ge(values_spread, 5)
                pe.wait_ge(loaded[last % 3], 16 * (last // 3 + 1))
                for c in range(4):
                    mm = nc.tensor.matmul(row_ps[:, :], spread[:, c, :], stage[:, last % 3, c, 0:BANK],
                                          start=c == 0, stop=c == 3)
                mm.then_inc(row_product, 1)


def layer_norm_program(nc, dve, s, g, eps, source, z, stats, mean_var, tick, stats_done, aggr_done,
                       eps_added, rstd_done, z_done):
    for b in range(GB):
        nc.vector.bn_stats(stats[:, b, :], source(b)).then_inc(stats_done, 1)
    dve.wait_ge(stats_done, plain(g, GB, GB - 1))
    nc.vector.memset(tick[:, 0:1], 0.0)
    for b in range(GB):
        nc.vector.bn_aggr(mean_var[:, b, 0:2], stats[:, b, :]).then_inc(aggr_done, 1)
    dve.wait_ge(aggr_done, plain(g, GB, GB - 1))
    nc.vector.tensor_scalar(mean_var[:, :, 2], mean_var[:, :, 1], eps, None, ALU.add).then_inc(eps_added, 1)
    for b in range(GB):
        if b == 0:
            dve.wait_ge(rstd_done, plain(g, 1, 0))
        nc.vector.tensor_scalar(z[:, b, :], source(b), mean_var[:, b, 0:1], mean_var[:, b, 3:4],
                                ALU.subtract, ALU.mult).then_inc(z_done, 1)


def attention_phase(nc, sems, s, name, X, ident, minus_half, *, cross, grouped, eps, ctx_in, mask_in, mask_multiplies,
                    mask_per_sequence, weights, bias_q, bias_k, bias_v, bias_o, ln_s, ln_b,
                    scale, finish):
    wq, wk, wv, wo = weights
    D, C, G = s.D, s.C, s.G
    kd = wk.shape[1]
    KJ = kd // P
    HD = 16 if grouped else 32
    KVH = kd // HD
    U = GB * (D // HD) // UH
    UB = U // GB
    HDV = HD + 1

    with ExitStack() as ctx:
        def sb(n, shape, dt=F32):
            return ctx.enter_context(nc.sbuf_tensor(f"{name}_{n}", shape, dt))

        def sem(n):
            return sems.named(n)

        Wq = [sb(f"Wq{h}", [P, C, D], F32R) for h in "hl"]
        Wk = [sb(f"Wk{h}", [P, C, kd], F32R) for h in "hl"]
        Wv = [sb(f"Wv{h}", [P, C, kd], F32R) for h in "hl"]
        Wo = [sb(f"Wo{h}", [P, C, D], F32R) for h in "hl"]
        row_bias = sb("row_bias", [P, D])
        if grouped:
            by_head = bias_v.rearrange("(c a d) -> a d c", a=2, d=HD)
            value_columns = [(i * HD, HD, by_head[i // 4, :, :]) for i in range(P // HD)]
        else:
            value_columns = [(0, P, column(bias_v))]
        prepare_weights(nc, sems, name, [
            (weight(wq), Wq[0][:, :, :], Wq[1][:, :, :]),
            (weight(wk), Wk[0][:, :, :], Wk[1][:, :, :]),
            (weight(wv), Wv[0][:, :, :], Wv[1][:, :, :]),
            (weight(wo), Wo[0][:, :, :], Wo[1][:, :, :]),
        ], D, rows=(value_columns, bias_o, row_bias))

        xT = [sb(f"xT{h}", [P, C, TOK], F32R) for h in "hl"]
        cT = [sb(f"cT{h}", [P, C, TOK], F32R) for h in "hl"] if cross else xT
        zs = sb("zs", [P, GB, D])
        if not grouped:
            affine = sb("affine", [P, 2, C, P])
            ln_cols = sb("ln_cols", [P, 2, C])
        stats = sb("stats", [P, GB, 6])
        tick = sb("tick", [P, 2])
        mean_var = sb("mean_var", [P, GB, 4])
        ctx_rows = sb("ctx_rows", [P, GB, D]) if cross else None
        qT = sb("qT", [P, C, TOK])
        if grouped:
            k_raw = sb("k_raw", [P, TOK])
            kT = sb("kT", [P, C, GB, 2, P])
        else:
            kT = sb("kT", [P, C, TOK])
        V = sb("V", [P, GB, KVH, HDV])
        t = sb("t", [P, 3, 2, 4, P])
        pT = sb("pT", [P, 2, 4, P])
        neg_max = sb("neg_max", [P, 2, UH])
        recip = sb("recip", [P, 2, UH])
        o_rows = sb("o_rows", [P, 2, D])
        oT = [sb(f"oT{h}", [P, C, P], F32R) for h in "hl"]
        NM = GB if mask_per_sequence else 1
        mask = sb("mask", [P, NM, P])
        mask_add = sb("mask_add", [P, NM, P]) if mask_multiplies else None
        bq = sb("bq", [P, C])
        bk = sb("bk", [P, KJ])
        if finish:
            y = sb("y", [P, 2, D])
            fstats = sb("fstats", [P, 2, 6])
            fmv = sb("fmv", [P, 2, 4])
            gamma = sb("gamma", [P, D])
            beta = sb("beta", [P, D])

        def psum(n, shape):
            return ctx.enter_context(nc.psum_tensor(f"{name}_{n}", shape, F32))

        ps = [psum(f"pair{i}", [P, 2, BANK]) for i in range(4)]

        def bank(i):
            return ps[i // 2][:, i % 2, :]

        small_in = sem("small_in")
        mask_loaded = sem("mask_loaded")
        ctx_loaded = sem("ctx_loaded")
        ones_set = sem("ones_set")
        rows_cleared = sem("rows_cleared")
        stats_done, aggr_done, eps_added, rstd_done, z_done = (
            sem(n) for n in ("stats_done", "aggr_done", "eps_added", "rstd_done", "z_done"))
        mask_ready = sem("mask_ready")
        row_added = sem("row_added")
        ctx_turned, x_turned = sem("ctx_turned"), sem("x_turned")
        c_high, c_low = sem("c_high"), sem("c_low")
        x_affine, x_high, x_low = sem("x_affine"), sem("x_high"), sem("x_low")
        k_made, q_made, v_made = sem("k_made"), sem("q_made"), sem("v_made")
        k_kept, q_kept, v_kept = sem("k_kept"), sem("q_kept"), sem("v_kept")
        k_placed = sem("k_placed")
        scores_made, scores_read, mask_added, max_done, probs_done = (
            sem(n) for n in ("scores_made", "scores_read", "mask_added", "max_done", "probs_done"))
        probs_turned, pT_a, pT_b = sem("probs_turned"), sem("pT_a"), sem("pT_b")
        out_made, recip_done, out_kept = sem("out_made"), sem("recip_done"), sem("out_kept")
        out_turned, o_high, o_low = sem("out_turned"), sem("o_high"), sem("o_low")
        final_made, x_added = sem("final_made"), sem("x_added")
        if finish:
            f_stats, f_aggr, f_eps, f_rstd, f_z, f_scaled, f_shifted = (
                sem(n) for n in ("f_stats", "f_aggr", "f_eps", "f_rstd", "f_z", "f_scaled", "f_shifted"))
            stored = [sem(f"stored{i}") for i in range(2)]

        X_BANK = 4 if cross else 0
        block = ctx.enter_context(nc.Block())

        def unit_heads(r, i):
            if not grouped:
                p, sl, c = r, i // 4, i % 4
                return sl, 2 * p + sl, c, 0
            p, cc = r % 2, r // 2
            sl, c2, e = i // 4, (i // 2) % 2, i % 2
            return sl, 2 * p + sl, 2 * cc + c2, e

        def value_head(quadrant, c, e):
            return 2 * c + quadrant // 2 if grouped else 4 * c + quadrant

        def load_context(eng, g):
            eng.wait_ge(ctx_turned, nth(g, GB, -1))
            eng.dma_start(ctx_rows[:, :, :],
                          ctx_in[bass.ds(g * GB, GB), :, :].rearrange("b p d -> p b d")).then_inc(ctx_loaded, 16)

        @block.sync
        def _(sp):
            if finish:
                for i in range(2):
                    sp.sem_inc(stored[i], 16)
            sp.dma_start(bq[:, :], column(bias_q), allow_slow_non_contiguous=True).then_inc(small_in, 16)
            sp.dma_start(bk[:, :], column(bias_k), allow_slow_non_contiguous=True).then_inc(small_in, 16)
            if not grouped:
                sp.dma_start(ln_cols[:, 0, :], column(ln_s), allow_slow_non_contiguous=True).then_inc(small_in, 16)
                sp.dma_start(ln_cols[:, 1, :], column(ln_b), allow_slow_non_contiguous=True).then_inc(small_in, 16)
            if finish:
                sp.dma_start(gamma[:, :], finish[0].partition_broadcast(P)).then_inc(small_in, 16)
                sp.dma_start(beta[:, :], finish[1].partition_broadcast(P)).then_inc(small_in, 16)
            if not mask_per_sequence:
                sp.dma_start(mask[:, 0, :], mask_in[0, 0, :, :]).then_inc(mask_loaded, 16)
            with sp.Fori(0, G) as g:
                if cross and not grouped:
                    load_context(sp, g)
                if mask_per_sequence:
                    sp.wait_ge(mask_added if mask_multiplies else scores_read, nth(g, U, -1))
                    sp.dma_start(mask[:, :, :], mask_in[bass.ds(g * GB, GB), 0, :, :].rearrange(
                        "b p k -> p b k")).then_inc(mask_loaded, 16)
                if grouped:
                    sp.wait_ge(k_kept, nth(g, 1, 0))
                    sp.wait_ge(scores_made, nth(g, U, -1))
                    sp.wait_ge(rows_cleared, 1)
                    for c in range(C):
                        for quadrant in range(4):
                            kv = 2 * c + quadrant // 2
                            for e in range(2):
                                row = QUAD * quadrant + HD * e
                                sp.dma_start(kT[row:row + HD, c, :, e, :],
                                             k_raw[HD * kv:HD * kv + HD, :].rearrange("p (b k) -> p b k", b=GB)
                                             ).then_inc(k_placed, 16)
                if finish:
                    for b in range(GB):
                        sp.wait_ge(f_shifted, plain(g, GB, b))
                        sp.dma_start(finish[3][bass.ds(g * GB + b, 1), :, :].rearrange("b p d -> p b d"),
                                     y[:, b % 2:b % 2 + 1, :]).then_inc(stored[b % 2], 16)
            if finish:
                for i in range(2):
                    sp.wait_ge(stored[i], 16 * (GB // 2 * G + 1))

        @block.gpsimd
        def _(pool):
            pool.sem_inc(row_added, AHEAD)
            pool.sem_inc(mask_added, AHEAD)
            if grouped:
                nc.gpsimd.memset(kT[:, :, :, :, :], 0.0).then_inc(rows_cleared, 1)
            with pool.Fori(0, G) as g:
                if grouped:
                    load_context(pool, g)
                else:
                    pool.wait_ge(eps_added, plain(g, 1, 0))
                    nc.gpsimd.tensor_tensor(mean_var[:, :, 3], mean_var[:, :, 2], minus_half[:, 0:GB],
                                            ALU.pow).then_inc(rstd_done, 1)
                for b in range(GB):
                    pool.wait_ge(z_done, nth(g, GB, b))
                    xb = X[:, bass.ds(g * GB + b, 1), :].rearrange("p b d -> p (b d)")
                    nc.gpsimd.tensor_tensor(xb, xb, row_bias[:, :], ALU.add).then_inc(row_added, 1)
                if mask_multiplies:
                    for u in range(U):
                        b = u // UB
                        pool.wait_ge(scores_read, nth(g, U, u))
                        if u == 0:
                            pool.wait_ge(mask_ready, plain(g if mask_per_sequence else 0, 1, 0))
                        m = b if mask_per_sequence else 0
                        tu = t[:, u % 3, :, :, :].rearrange("p a c k -> p (a c) k")
                        nc.gpsimd.tensor_tensor(tu, tu, mask_add[:, m:m + 1, :].to_broadcast([P, UH, P]),
                                                ALU.add).then_inc(mask_added, 1)
                if finish:
                    for b in range(GB):
                        pool.wait_ge(f_eps, plain(g, GB, b))
                        nc.gpsimd.tensor_tensor(fmv[:, b % 2, 3:4], fmv[:, b % 2, 2:3], minus_half[:, 0:1],
                                                ALU.pow).then_inc(f_rstd, 1)
                        pool.wait_ge(f_z, plain(g, GB, b))
                        yb = y[:, b % 2, :]
                        nc.gpsimd.tensor_tensor(yb, yb, gamma[:, :], ALU.mult).then_inc(f_scaled, 1)
                        pool.wait_ge(f_scaled, plain(g, GB, b))
                        nc.gpsimd.tensor_tensor(yb, yb, beta[:, :], ALU.add).then_inc(f_shifted, 1)

        @block.scalar
        def _(act):
            for done in (c_high, x_affine, k_kept, v_kept, probs_done, pT_a, o_high):
                act.sem_inc(done, AHEAD)
            if grouped:
                act.sem_inc(x_high, AHEAD)
            act.wait_ge(small_in, 16 * 4)
            with act.Fori(0, G) as g:
                if cross:
                    for b in range(GB):
                        act.wait_ge(ctx_turned, nth(g, GB, b))
                        if b == 0:
                            act.wait_ge(v_made, nth(g, GB, -1))
                        nc.scalar.copy(cT[0][:, :, b * P:(b + 1) * P],
                                       bank(b).rearrange("p (c k) -> p c k", c=C)).then_inc(c_high, 1)
                for b in range(GB):
                    act.wait_ge(x_turned, nth(g, GB, b))
                    src = bank(X_BANK + b)
                    if grouped:
                        if b == 0:
                            act.wait_ge(q_made, nth(g, C, -1))
                        nc.scalar.copy(xT[0][:, :, b * P:(b + 1) * P],
                                       src.rearrange("p (c k) -> p c k", c=C)).then_inc(x_high, 1)
                    else:
                        act.wait_ge(x_low, nth(g, GB, b - 2))
                        for c in range(C):
                            nc.scalar.activation(affine[:, b % 2, c, :], src[:, c * P:(c + 1) * P], ACT.Identity,
                                                 bias=ln_cols[:, 1, c:c + 1], scale=ln_cols[:, 0, c:c + 1]
                                                 ).then_inc(x_affine, 1)
                for m in range(KJ):
                    act.wait_ge(k_made, nth(g, KJ, m))
                    if m == 0:
                        act.wait_ge(scores_made, nth(g, U, -1))
                    dst = k_raw[:, :] if grouped else kT[:, m, :]
                    nc.scalar.activation(dst, bank(m), ACT.Identity, bias=bk[:, m:m + 1]).then_inc(k_kept, 1)

                def keep_values(b):
                    act.wait_ge(v_made, nth(g, GB, b))
                    if b == 0:
                        act.wait_ge(out_made, nth(g, U, -1))
                        act.wait_ge(ones_set, 1)
                    src = bank((6, 7, 4, 5)[b])[:, 0:kd].rearrange("p (h d) -> p h d", h=KVH)
                    nc.scalar.copy(V[:, b, :, 0:HD], src).then_inc(v_kept, 1)

                def probabilities(u):
                    act.wait_ge(max_done, nth(g, U, u))
                    tu = t[:, u % 3, :, :, :].rearrange("p a c k -> p (a c) k")
                    for i in range(UH):
                        nc.scalar.activation(tu[:, i, :], tu[:, i, :], ACT.Exp,
                                             bias=neg_max[:, u % 2, i:i + 1]).then_inc(probs_done, 1)

                keep_values(0)
                keep_values(1)
                probabilities(0)
                keep_values(2)
                keep_values(3)
                probabilities(1)
                for u in range(U):
                    act.wait_ge(probs_turned, nth(g, 2 * U, 2 * u))
                    act.wait_ge(out_made, nth(g, U, u - 1))
                    nc.scalar.copy(pT[:, 0, :, :], bank(4).rearrange("p (c k) -> p c k", c=4)).then_inc(pT_a, 1)
                    if u % UB == 0 and u > 0:
                        b = u // UB - 1
                        act.wait_ge(out_turned, nth(g, GB, b))
                        act.wait_ge(final_made, nth(g, GB, b - 1))
                        nc.scalar.copy(oT[0][:, :, :], bank(7).rearrange("p (c k) -> p c k", c=C)).then_inc(o_high, 1)
                    if u + 2 < U:
                        probabilities(u + 2)
                act.wait_ge(out_turned, nth(g, GB, GB - 1))
                act.wait_ge(final_made, nth(g, GB, GB - 2))
                nc.scalar.copy(oT[0][:, :, :], bank(7).rearrange("p (c k) -> p c k", c=C)).then_inc(o_high, 1)

        @block.vector
        def _(dve):
            for done in (c_low, x_low, q_kept, scores_read, max_done, pT_b, out_kept, o_low, x_added, z_done):
                dve.sem_inc(done, AHEAD)
            if not grouped:
                dve.sem_inc(x_high, AHEAD)
            nc.vector.memset(V[:, :, :, HD:HDV], 1.0).then_inc(ones_set, 1)
            dve.wait_ge(small_in, 16 * 4)
            if mask_multiplies and not mask_per_sequence:
                dve.wait_ge(mask_loaded, 16)
                nc.vector.tensor_scalar(mask_add[:, :, :], mask[:, :, :], 1.0, 10000.0,
                                        ALU.subtract, ALU.mult).then_inc(mask_ready, 1)
            with dve.Fori(0, G) as g:
                def x_row(b):
                    return X[:, bass.ds(g * GB + b, 1), :].rearrange("p b d -> p (b d)")

                dve.wait_ge(x_turned, nth(g, GB, -1))
                if grouped:
                    for b in range(GB):
                        nc.vector.tensor_copy(zs[:, b, :], x_row(b)).then_inc(z_done, 1)
                else:
                    layer_norm_program(nc, dve, s, g, eps, x_row, zs, stats, mean_var, tick, stats_done, aggr_done,
                                       eps_added, rstd_done, z_done)
                if mask_multiplies and mask_per_sequence:
                    dve.wait_ge(mask_loaded, 16 * g + 16)
                    dve.wait_ge(mask_added, nth(g, U, -1))
                    nc.vector.tensor_scalar(mask_add[:, :, :], mask[:, :, :], 1.0, 10000.0,
                                            ALU.subtract, ALU.mult).then_inc(mask_ready, 1)
                if cross:
                    for b in range(GB):
                        dve.wait_ge(c_high, nth(g, GB, b))
                        tok = slice(b * P, (b + 1) * P)
                        nc.vector.tensor_tensor(cT[1][:, :, tok], bank(b).rearrange("p (c k) -> p c k", c=C),
                                                cT[0][:, :, tok].bitcast(F32), ALU.subtract).then_inc(c_low, 1)
                for b in range(GB):
                    tok = slice(b * P, (b + 1) * P)
                    if grouped:
                        dve.wait_ge(x_high, nth(g, GB, b))
                        nc.vector.tensor_tensor(xT[1][:, :, tok], bank(X_BANK + b).rearrange("p (c k) -> p c k", c=C),
                                                xT[0][:, :, tok].bitcast(F32), ALU.subtract).then_inc(x_low, 1)
                    else:
                        dve.wait_ge(x_affine, nth(g, GB * C, b * C + C - 1))
                        if b == 0:
                            dve.wait_ge(q_made, nth(g, C, -1))
                            if not cross:
                                dve.wait_ge(v_made, nth(g, GB, -1))
                        nc.vector.tensor_copy(xT[0][:, :, tok], affine[:, b % 2, :, :]).then_inc(x_high, 1)
                        dve.wait_ge(x_high, nth(g, GB, b))
                        nc.vector.tensor_tensor(xT[1][:, :, tok], affine[:, b % 2, :, :],
                                                xT[0][:, :, tok].bitcast(F32), ALU.subtract).then_inc(x_low, 1)
                for m in range(C):
                    dve.wait_ge(q_made, nth(g, C, m))
                    if m == 0:
                        dve.wait_ge(scores_made, nth(g, U, -1))
                    nc.vector.tensor_scalar(qT[:, m, :], bank(4 + m), bq[:, m:m + 1], scale,
                                            ALU.add, ALU.mult).then_inc(q_kept, 1)

                def read_scores(u):
                    dve.wait_ge(scores_made, nth(g, U, u))
                    if u >= 3:
                        dve.wait_ge(probs_turned, nth(g, 2 * U, 2 * (u - 3) + 1))
                    else:
                        dve.wait_ge(probs_turned, nth(g, 2 * U, -1))
                    b = u // UB if mask_per_sequence else 0
                    if u == 0 and mask_per_sequence:
                        dve.wait_ge(mask_loaded, 16 * g + 16)
                    sc = ps[u % 2][:, :, :].rearrange("p a (c k) -> p (a c) k", k=P)
                    tu = t[:, u % 3, :, :, :].rearrange("p a c k -> p (a c) k")
                    nc.vector.tensor_tensor(tu, sc, mask[:, b:b + 1, :].to_broadcast([P, UH, P]),
                                            ALU.mult if mask_multiplies else ALU.add).then_inc(scores_read, 1)

                def row_max(u):
                    if mask_multiplies:
                        dve.wait_ge(mask_added, nth(g, U, u))
                    else:
                        dve.wait_ge(scores_read, nth(g, U, u))
                    if u >= 2:
                        dve.wait_ge(probs_done, nth(g, U * UH, (u - 2) * UH + UH - 1))
                    else:
                        dve.wait_ge(probs_done, nth(g, U * UH, -1))
                    tu = t[:, u % 3, :, :, :].rearrange("p a c k -> p (a c) k")
                    nc.vector.tensor_reduce(neg_max[:, u % 2, :], tu, AX.X, ALU.max,
                                            negate=True).then_inc(max_done, 1)

                def keep_output(u):
                    b, r = u // UB, u % UB
                    dve.wait_ge(out_made, nth(g, U, u))
                    o = bank(6)[:, 0:UH * HDV].rearrange("p (i d) -> p i d", i=UH)
                    nc.vector.reciprocal(recip[:, u % 2, :], o[:, :, HD]).then_inc(recip_done, 1)
                    dve.wait_ge(recip_done, plain(g, U, u))
                    if r == 0:
                        dve.wait_ge(out_turned, nth(g, GB, b - 2))
                    if not grouped:
                        dst = o_rows[:, b % 2, :].rearrange("p (c j d) -> p j c d", c=C, j=4)[:, 2 * r:2 * r + 2, :, :]
                        nc.vector.tensor_tensor(
                            dst, o[:, :, 0:HD].rearrange("p (a c) d -> p a c d", a=2),
                            recip[:, u % 2, :].rearrange("p (a c) -> p a c", a=2).unsqueeze(3).to_broadcast([P, 2, C, HD]),
                            ALU.mult).then_inc(out_kept, 1)
                    else:
                        p, cc = r % 2, r // 2
                        for sl in range(2):
                            q = 2 * p + sl
                            dst = o_rows[:, b % 2, :].rearrange("p (c j e d) -> p c j e d", c=C, j=4, e=2)[
                                :, 2 * cc:2 * cc + 2, q, :, :]
                            src = o[:, 4 * sl:4 * sl + 4, 0:HD].rearrange("p (c e) d -> p c e d", c=2)
                            rec = recip[:, u % 2, 4 * sl:4 * sl + 4].rearrange("p (c e) -> p c e", c=2).unsqueeze(3)
                            ins = nc.vector.tensor_tensor(dst, src, rec.to_broadcast([P, 2, 2, HD]), ALU.mult)
                        ins.then_inc(out_kept, 1)

                def output_low(b):
                    dve.wait_ge(o_high, nth(g, GB, b))
                    nc.vector.tensor_tensor(oT[1][:, :, :], bank(7).rearrange("p (c k) -> p c k", c=C),
                                            oT[0][:, :, :].bitcast(F32), ALU.subtract).then_inc(o_low, 1)

                def add_output(b):
                    dve.wait_ge(final_made, nth(g, GB, b))
                    dve.wait_ge(row_added, nth(g, GB, b))
                    if not finish:
                        nc.vector.tensor_tensor(x_row(b), bank(7), x_row(b), ALU.add).then_inc(x_added, 1)
                        return
                    yb = y[:, b % 2, :]
                    finish_row(b, yb)

                def finish_row(b, yb):
                    i = b % 2
                    dve.wait_ge(stored[i], 16 * (g * 2 + b // 2) + 16)
                    nc.vector.tensor_tensor(yb, bank(7), x_row(b), ALU.add).then_inc(x_added, 1)
                    dve.wait_ge(x_added, nth(g, GB, b))
                    nc.vector.bn_stats(fstats[:, i, :], yb).then_inc(f_stats, 1)
                    dve.wait_ge(f_stats, plain(g, GB, b))
                    nc.vector.memset(tick[:, i:i + 1], 0.0)
                    nc.vector.bn_aggr(fmv[:, i, 0:2], fstats[:, i, :]).then_inc(f_aggr, 1)
                    dve.wait_ge(f_aggr, plain(g, GB, b))
                    nc.vector.tensor_scalar(fmv[:, i, 2:3], fmv[:, i, 1:2], finish[2], None, ALU.add).then_inc(f_eps, 1)
                    dve.wait_ge(f_rstd, plain(g, GB, b))
                    nc.vector.tensor_scalar(yb, yb, fmv[:, i, 0:1], fmv[:, i, 3:4], ALU.subtract,
                                            ALU.mult).then_inc(f_z, 1)

                read_scores(0)
                read_scores(1)
                row_max(0)
                row_max(1)
                for u in range(U):
                    dve.wait_ge(probs_turned, nth(g, 2 * U, 2 * u + 1))
                    dve.wait_ge(out_made, nth(g, U, u - 1))
                    nc.vector.tensor_copy(pT[:, 1, :, :], bank(5).rearrange("p (c k) -> p c k", c=4)).then_inc(pT_b, 1)
                    if u + 2 < U:
                        read_scores(u + 2)
                    if u % UB == 0 and u > 0:
                        output_low(u // UB - 1)
                    keep_output(u)
                    if u + 2 < U:
                        row_max(u + 2)
                    if u % UB == 0 and u > 0:
                        add_output(u // UB - 1)
                output_low(GB - 1)
                add_output(GB - 1)

        @block.tensor
        def _(pe):
            for done in (ctx_turned, x_turned, k_made, q_made, v_made, scores_made, probs_turned, out_made,
                         out_turned, final_made):
                pe.sem_inc(done, AHEAD)
            pe.wait_ge(ones_set, 1)
            with pe.Fori(0, G) as g:
                if cross:
                    pe.wait_ge(ctx_loaded, 16 * g + 16)
                    pe.wait_ge(scores_read, nth(g, U, -1))
                    for b in range(GB):
                        for c in range(C):
                            mm = nc.tensor.transpose(bank(b)[:, c * P:(c + 1) * P], ctx_rows[:, b, c * P:(c + 1) * P],
                                                     ident[:, :])
                        mm.then_inc(ctx_turned, 1)
                pe.wait_ge(scores_read, nth(g, U, -1))
                pe.wait_ge(pT_a, nth(g, U, -1))
                pe.wait_ge(pT_b, nth(g, U, -1))
                pe.wait_ge(out_kept, nth(g, U, -1))
                pe.wait_ge(x_added, nth(g, GB, -1))
                for b in range(GB):
                    pe.wait_ge(z_done, nth(g, GB, b))
                    for c in range(C):
                        mm = nc.tensor.transpose(bank(X_BANK + b)[:, c * P:(c + 1) * P], zs[:, b, c * P:(c + 1) * P],
                                                 ident[:, :])
                    mm.then_inc(x_turned, 1)

                def project(out, stationary, moving):
                    for c in range(C):
                        for n, (a, b) in enumerate(((1, 0), (0, 1), (0, 0))):
                            mm = nc.tensor.matmul(out, stationary(c, a), moving(c, b),
                                                  start=c == 0 and n == 0, stop=c == C - 1 and n == 2)
                    return mm

                if cross:
                    pe.wait_ge(c_low, nth(g, GB, GB - 1))
                else:
                    pe.wait_ge(x_low, nth(g, GB, GB - 1))
                for m in range(KJ):
                    project(bank(m), lambda c, h: Wk[h][:, c, m * P:(m + 1) * P],
                            lambda c, h: cT[h][:, c, :]).then_inc(k_made, 1)
                pe.wait_ge(x_low, nth(g, GB, GB - 1))
                for m in range(C):
                    project(bank(4 + m), lambda c, h: Wq[h][:, c, m * P:(m + 1) * P],
                            lambda c, h: xT[h][:, c, :]).then_inc(q_made, 1)

                def scores(u):
                    b, r = u // UB, u % UB
                    if u >= 2:
                        pe.wait_ge(scores_read, nth(g, U, u - 2))
                    if u == 0:
                        pe.wait_ge(k_kept, nth(g, KJ, KJ - 1))
                        pe.wait_ge(q_kept, nth(g, C, C - 1))
                        if grouped:
                            pe.wait_ge(k_placed, 16 * 32 * g + 16 * 32)
                    tok = slice(b * P, (b + 1) * P)
                    pair = ps[u % 2]
                    for i in (0, 4, 1, 5, 2, 6, 3, 7):
                        sl, q, c, e = unit_heads(r, i)
                        rows = slice(QUAD * q, QUAD * q + QUAD)
                        if not grouped:
                            mm = nc.tensor.matmul(pair[:, sl, c * P:(c + 1) * P], qT[rows, c, tok], kT[rows, c, tok],
                                                  start=True, stop=True)
                        elif e == 0:
                            at = (i // 2) % 2 * 2 * P
                            mm = nc.tensor.matmul(pair[:, sl, at:at + 2 * P], qT[rows, c, tok],
                                                  kT[rows, c, b, :, :].rearrange("p e k -> p (e k)"),
                                                  start=True, stop=True)
                    mm.then_inc(scores_made, 1)

                def values(b):
                    if b == 0:
                        pe.wait_ge(q_kept, nth(g, C, C - 1))
                    project(bank((6, 7, 4, 5)[b])[:, 0:kd], lambda c, h: cT[h][:, c, b * P:(b + 1) * P],
                            lambda c, h: Wv[h][:, c, :]).then_inc(v_made, 1)

                def turn_probs(u):
                    tu = t[:, u % 3, :, :, :]
                    for sl in range(2):
                        pe.wait_ge(probs_done, nth(g, U * UH, u * UH + 4 * sl + 3))
                        if sl == 0:
                            pe.wait_ge(v_kept, nth(g, GB, GB - 1)) if u == 0 else pe.wait_ge(pT_a, nth(g, U, u - 1))
                        elif u:
                            pe.wait_ge(pT_b, nth(g, U, u - 1))
                        for c in range(4):
                            mm = nc.tensor.transpose(bank(4 + sl)[:, c * P:(c + 1) * P], tu[:, sl, c, :], ident[:, :])
                        mm.then_inc(probs_turned, 1)

                def outputs(u):
                    b, r = u // UB, u % UB
                    pe.wait_ge(pT_a, nth(g, U, u))
                    if u:
                        pe.wait_ge(out_kept, nth(g, U, u - 1))
                    for i in range(UH):
                        if i == 4:
                            pe.wait_ge(pT_b, nth(g, U, u))
                        sl, q, c, e = unit_heads(r, i)
                        mm = nc.tensor.matmul(bank(6)[:, i * HDV:(i + 1) * HDV], pT[:, sl, i % 4, :],
                                              V[:, b, value_head(q, c, e), :], start=True, stop=True)
                    mm.then_inc(out_made, 1)

                def turn_output(b):
                    pe.wait_ge(out_kept, nth(g, U, (b + 1) * UB - 1))
                    if b:
                        pe.wait_ge(x_added, nth(g, GB, b - 1))
                    for c in range(C):
                        mm = nc.tensor.transpose(bank(7)[:, c * P:(c + 1) * P], o_rows[:, b % 2, c * P:(c + 1) * P],
                                                 ident[:, :])
                    mm.then_inc(out_turned, 1)

                def project_output(b):
                    pe.wait_ge(o_low, nth(g, GB, b))
                    project(bank(7), lambda c, h: oT[h][:, c, :], lambda c, h: Wo[h][:, c, :]).then_inc(final_made, 1)

                scores(0)
                values(0)
                values(1)
                scores(1)
                values(2)
                values(3)
                for u in range(U):
                    turn_probs(u)
                    if u + 2 < U:
                        scores(u + 2)
                    if u % UB == 0 and u > 0:
                        turn_output(u // UB - 1)
                    outputs(u)
                    if u % UB == 0 and u > 0:
                        project_output(u // UB - 1)
                turn_output(GB - 1)
                project_output(GB - 1)


def mlp_phase(nc, sems, s, X, ident, minus_half, *, eps, w1, b1, w2, b2, ln_s, ln_b):
    D, C, G, M = s.D, s.C, s.G, s.M
    with ExitStack() as ctx:
        def sb(n, shape, dt=F32):
            return ctx.enter_context(nc.sbuf_tensor(f"mlp_{n}", shape, dt))

        def sem(n):
            return sems.named(n)

        W1 = [sb(f"W1{h}", [P, C, s.F], F32R) for h in "hl"]
        W2 = [sb(f"W2{h}", [P, M, D], F32R) for h in "hl"]
        w2v = weight(w2)
        prepare_weights(nc, sems, "mlp", [
            (weight(w1)[:, :, n:n + D], W1[0][:, :, n:n + D], W1[1][:, :, n:n + D]) for n in range(0, s.F, D)
        ] + [(w2v[:, k:k + 4, :], W2[0][:, k:k + 4, :], W2[1][:, k:k + 4, :]) for k in range(0, M, 4)], D)

        xT = [sb(f"xT{h}", [P, C, TOK], F32R) for h in "hl"]
        zs = sb("zs", [P, GB, D])
        affine = sb("affine", [P, 1, C, P])
        ln_cols = sb("ln_cols", [P, 2, C])
        b1_cols = sb("b1_cols", [P, M])
        row_bias = sb("row_bias", [P, D])
        stats = sb("stats", [P, GB, 6])
        tick = sb("tick", [P, 2])
        mean_var = sb("mean_var", [P, GB, 4])
        hidden = sb("hidden", [P, 2, TOK])
        hT = [sb(f"hT{h}", [P, 2, TOK], F32R) for h in "hl"]
        acc = ctx.enter_context(nc.psum_tensor("mlp_acc", [P, GB, BANK], F32))
        work = ctx.enter_context(nc.psum_tensor("mlp_work", [P, 4, BANK], F32))

        small_in = sem("small_in")
        stats_done, aggr_done, eps_added, rstd_done, z_done = (
            sem(n) for n in ("stats_done", "aggr_done", "eps_added", "rstd_done", "z_done"))
        row_added, x_turned, x_affine, x_high, x_low = (
            sem(n) for n in ("row_added", "x_turned", "x_affine", "x_high", "x_low"))
        hidden_made, gelu_done, h_high, h_low, sums_made, x_added = (
            sem(n) for n in ("hidden_made", "gelu_done", "h_high", "h_low", "sums_made", "x_added"))
        chunk_used = sem("chunk_used")
        block = ctx.enter_context(nc.Block())

        @block.sync
        def _(sp):
            sp.dma_start(ln_cols[:, 0, :], column(ln_s), allow_slow_non_contiguous=True).then_inc(small_in, 16)
            sp.dma_start(ln_cols[:, 1, :], column(ln_b), allow_slow_non_contiguous=True).then_inc(small_in, 16)
            sp.dma_start(b1_cols[:, :], column(b1), allow_slow_non_contiguous=True).then_inc(small_in, 16)
            sp.dma_start(row_bias[:, :], b2.partition_broadcast(P)).then_inc(small_in, 16)

        @block.gpsimd
        def _(pool):
            pool.sem_inc(h_low, AHEAD)
            pool.wait_ge(small_in, 16 * 4)
            with pool.Fori(0, G) as g:
                pool.wait_ge(eps_added, plain(g, 1, 0))
                nc.gpsimd.tensor_tensor(mean_var[:, :, 3], mean_var[:, :, 2], minus_half[:, 0:GB],
                                        ALU.pow).then_inc(rstd_done, 1)
                for b in range(GB):
                    pool.wait_ge(z_done, plain(g, GB, b))
                    xb = X[:, bass.ds(g * GB + b, 1), :].rearrange("p b d -> p (b d)")
                    nc.gpsimd.tensor_tensor(xb, xb, row_bias[:, :], ALU.add).then_inc(row_added, 1)

        @block.scalar
        def _(act):
            act.sem_inc(gelu_done, AHEAD)
            act.wait_ge(small_in, 16 * 4)
            with act.Fori(0, G) as g:
                for b in range(GB):
                    act.wait_ge(x_turned, nth(g, GB, b))
                    act.wait_ge(x_low, nth(g, GB, b - 1))
                    for c in range(C):
                        nc.scalar.activation(affine[:, 0, c, :], work[:, b, c * P:(c + 1) * P], ACT.Identity,
                                             bias=ln_cols[:, 1, c:c + 1], scale=ln_cols[:, 0, c:c + 1]
                                             ).then_inc(x_affine, 1)
                for m in range(M):
                    act.wait_ge(hidden_made, plain(g, M, m))
                    act.wait_ge(h_low, nth(g, M, m - 2))
                    nc.scalar.activation(hidden[:, m % 2, :], work[:, m % 2, :], ACT.Gelu_apprx_tanh,
                                         bias=b1_cols[:, m:m + 1]).then_inc(gelu_done, 1)

        @block.vector
        def _(dve):
            for done in (x_low, x_added):
                dve.sem_inc(done, AHEAD)
            with dve.Fori(0, G) as g:
                def x_row(b):
                    return X[:, bass.ds(g * GB + b, 1), :].rearrange("p b d -> p (b d)")

                dve.wait_ge(x_turned, nth(g, GB, -1))
                layer_norm_program(nc, dve, s, g, eps, x_row, zs, stats, mean_var, tick, stats_done, aggr_done,
                                   eps_added, rstd_done, z_done)
                for b in range(GB):
                    tok = slice(b * P, (b + 1) * P)
                    dve.wait_ge(x_affine, plain(g, GB * C, b * C + C - 1))
                    nc.vector.tensor_copy(xT[0][:, :, tok], affine[:, 0, :, :]).then_inc(x_high, 1)
                    dve.wait_ge(x_high, plain(g, GB, b))
                    nc.vector.tensor_tensor(xT[1][:, :, tok], affine[:, 0, :, :],
                                            xT[0][:, :, tok].bitcast(F32), ALU.subtract).then_inc(x_low, 1)
                for m in range(M):
                    dve.wait_ge(gelu_done, nth(g, M, m))
                    dve.wait_ge(chunk_used, nth(g, M, m - 2))
                    nc.vector.tensor_copy(hT[0][:, m % 2, :], hidden[:, m % 2, :]).then_inc(h_high, 1)
                    dve.wait_ge(h_high, plain(g, M, m))
                    nc.vector.tensor_tensor(hT[1][:, m % 2, :], hidden[:, m % 2, :],
                                            hT[0][:, m % 2, :].bitcast(F32), ALU.subtract).then_inc(h_low, 1)
                for b in range(GB):
                    dve.wait_ge(row_added, plain(g, GB, b))
                    dve.wait_ge(chunk_used, nth(g, M, M - 1))
                    nc.vector.tensor_tensor(x_row(b), acc[:, b, :], x_row(b), ALU.add).then_inc(x_added, 1)

        @block.tensor
        def _(pe):
            for done in (x_turned, chunk_used):
                pe.sem_inc(done, AHEAD)
            with pe.Fori(0, G) as g:
                pe.wait_ge(gelu_done, nth(g, M, -1))
                for b in range(GB):
                    pe.wait_ge(z_done, plain(g, GB, b))
                    for c in range(C):
                        mm = nc.tensor.transpose(work[:, b, c * P:(c + 1) * P], zs[:, b, c * P:(c + 1) * P],
                                                 ident[:, :])
                    mm.then_inc(x_turned, 1)

                def hidden_chunk(m):
                    if m == 0:
                        pe.wait_ge(x_low, nth(g, GB, GB - 1))
                    if m >= 2:
                        pe.wait_ge(gelu_done, nth(g, M, m - 2))
                    for c in range(C):
                        for n, (a, b) in enumerate(((1, 0), (0, 1), (0, 0))):
                            mm = nc.tensor.matmul(work[:, m % 2, :], W1[a][:, c, m * P:(m + 1) * P], xT[b][:, c, :],
                                                  start=c == 0 and n == 0, stop=c == C - 1 and n == 2)
                    mm.then_inc(hidden_made, 1)

                hidden_chunk(0)
                hidden_chunk(1)
                for m in range(M):
                    pe.wait_ge(h_low, nth(g, M, m))
                    if m == 0:
                        pe.wait_ge(x_added, nth(g, GB, -1))
                    for b in range(GB):
                        tok = slice(b * P, (b + 1) * P)
                        for n, (ha, hb) in enumerate(((1, 0), (0, 1), (0, 0))):
                            mm = nc.tensor.matmul(acc[:, b, :], hT[ha][:, m % 2, tok], W2[hb][:, m, :],
                                                  start=m == 0 and n == 0, stop=m == M - 1 and n == 2)
                    mm.then_inc(chunk_used, 1)
                    if m + 2 < M:
                        hidden_chunk(m + 2)


def load_residual(nc, sems, s, x, X, ident, minus_half):
    with ExitStack() as ctx:
        x_in = sems.named("x_in")
        set_up = sems.named("set_up")
        block = ctx.enter_context(nc.Block())

        @block.sync
        def _(sp):
            for g in range(s.G):
                sp.dma_start(X[:, g * GB:(g + 1) * GB, :],
                             x[g * GB:(g + 1) * GB, :, :].rearrange("b p d -> p b d")).then_inc(x_in, 16)
            sp.wait_ge(x_in, 16 * s.G)

        @block.gpsimd
        def _(pool):
            nc.gpsimd.memset(ident[:, :], 0.0).then_inc(set_up, 1)
            nc.gpsimd.memset(minus_half[:, :], -0.5).then_inc(set_up, 1)
            pool.wait_ge(set_up, 2)
            nc.gpsimd.affine_select(out=ident[:, :], in_=ident[:, :], compare_op=ALU.not_equal, fill=1.0, base=0,
                                    pattern=[[-1, P]], channel_multiplier=1).then_inc(set_up, 1)
            pool.wait_ge(set_up, 3)


def build_cross_attention_layers(nc, a, out):
    s = Shape(a["x"], a["L0_xattn_w1"])
    D = s.D
    with ExitStack() as ctx:
        sems = Semaphores(nc, ctx)
        X = ctx.enter_context(nc.sbuf_tensor("X", [P, s.NB, D], F32))
        ident = ctx.enter_context(nc.sbuf_tensor("ident", [P, P], F32))
        minus_half = ctx.enter_context(nc.sbuf_tensor("minus_half", [P, GB], F32))
        load_residual(nc, sems, s, a["x"], X, ident, minus_half)
        w_qkv, b_qkv = a["L0_xattn_w_qkv"], a["L0_xattn_b_qkv"]
        attention_phase(
            nc, sems, s, "self", X, ident, minus_half, cross=False, grouped=False, eps=1e-5, ctx_in=None,
            mask_in=a["mask_1x1xSxS2_fc1"], mask_multiplies=True, mask_per_sequence=False,
            weights=(w_qkv[:, 0:D], w_qkv[:, D:2 * D], w_qkv[:, 2 * D:3 * D], a["L0_xattn_w_ao"]),
            bias_q=b_qkv[0:D], bias_k=b_qkv[D:2 * D], bias_v=b_qkv[2 * D:3 * D], bias_o=a["L0_xattn_b_ao"],
            ln_s=a["L0_xattn_ln1_s"], ln_b=a["L0_xattn_ln1_b"], scale=32 ** -0.5, finish=None)
        sems.clear()
        w_kv, b_kv = a["L0_xattn_w_kv"], a["L0_xattn_b_kv"]
        attention_phase(
            nc, sems, s, "cross", X, ident, minus_half, cross=True, grouped=False, eps=1e-5, ctx_in=a["ctx_2048"],
            mask_in=a["mask_Bx1xSxS2_ff1"], mask_multiplies=True, mask_per_sequence=True,
            weights=(a["L0_xattn_w_q"], w_kv[:, 0:D], w_kv[:, D:2 * D], a["L0_xattn_w_co"]),
            bias_q=a["L0_xattn_b_q"], bias_k=b_kv[0:D], bias_v=b_kv[D:2 * D], bias_o=a["L0_xattn_b_co"],
            ln_s=a["L0_xattn_ln2_s"], ln_b=a["L0_xattn_ln2_b"], scale=32 ** -0.5, finish=None)
        sems.clear()
        mlp_phase(nc, sems, s, X, ident, minus_half, eps=1e-5, w1=a["L0_xattn_w1"], b1=a["L0_xattn_b1"],
                  w2=a["L0_xattn_w2"], b2=a["L0_xattn_b2"], ln_s=a["L0_xattn_ln3_s"], ln_b=a["L0_xattn_ln3_b"])
        sems.clear()
        attention_phase(
            nc, sems, s, "grouped", X, ident, minus_half, cross=True, grouped=True, eps=None, ctx_in=a["ctx_2048"],
            mask_in=a["mask_Bx1xSxS2_ff0"], mask_multiplies=False, mask_per_sequence=True,
            weights=(a["L1_xattn_Wq"], a["L1_xattn_Wk"], a["L1_xattn_Wv"], a["L1_xattn_Wo"]),
            bias_q=a["L1_xattn_bq"], bias_k=a["L1_xattn_bk"], bias_v=a["L1_xattn_bv"], bias_o=a["L1_xattn_bo"],
            ln_s=None, ln_b=None, scale=16 ** -0.5,
            finish=(a["L1_xattn_gamma"], a["L1_xattn_beta"], 1e-6, out))


def kernel(**inputs):
    import numpy as np
    import concourse.bacc as bacc
    from concourse.bass_utils import run_bass_kernel_spmd

    nc = bacc.Bacc("TRN2", target_bir_lowering=False, num_devices=1)
    arrays, args = {}, {}
    for name, value in inputs.items():
        a = np.ascontiguousarray(value)
        arrays[f"in_{name}_dram"] = a
        args[name] = nc.dram_tensor(f"in_{name}_dram", a.shape, mybir.dt.from_np(a.dtype), kind="ExternalInput").ap()
    x = arrays["in_x_dram"]
    out = nc.dram_tensor("out_dram", x.shape, mybir.dt.from_np(x.dtype), kind="ExternalOutput").ap()
    build_cross_attention_layers(nc, args, out)
    r = run_bass_kernel_spmd(nc, [arrays], core_ids=[0])
    return r.results[0]["out_dram"]
```

```python
from contextlib import ExitStack

import concourse.bass as bass
from concourse import mybir

F32 = mybir.dt.float32
F32R = mybir.dt.float32r
ALU = mybir.AluOpType
ACT = mybir.ActivationFunctionType
AX = mybir.AxisListType

P = 128
QUAD = 32
GB = 2
TOK = GB * P
BANK = 512
UH = 8


AHEAD = 24


def at(n):
    return n + (1 + AHEAD)


def over_groups(eng, count, body):
    with eng.Fori(0, count // 2 - 1) as i:
        body(2 * i, 0, 2)
        body(2 * i + 1, 1, 2)
    body(count - 2, 0, 1)
    body(count - 1, 1, 0)


class Semaphores:

    def __init__(self, nc, ctx):
        self.nc, self.ctx, self.by_name = nc, ctx, {}

    def named(self, name):
        if name not in self.by_name:
            self.by_name[name] = self.ctx.enter_context(self.nc.semaphore(name))
        return self.by_name[name]

    def clear(self):
        with self.nc.Block() as block:
            @block.sync
            def _(sp):
                for done in self.by_name.values():
                    sp.sem_clear(done)


class Shape:

    def __init__(self, x, w1):
        self.NB, self.S, self.D = x.shape
        self.C = self.D // P
        self.G = self.NB // GB
        self.F = w1.shape[1]
        self.M = self.F // P


def column(v):
    return v.rearrange("(c p) -> p c", p=P)


def weight(w):
    return w.rearrange("(k p) n -> p k n", p=P)


def prepare_weights(nc, sems, name, units, stage_cols, rows=None):
    with ExitStack() as ctx:
        stage = ctx.enter_context(nc.sbuf_tensor(f"{name}_stage", [P, 3, 4, stage_cols], F32))
        loaded = [sems.named(f"loaded{i}") for i in range(3)]
        high_done = sems.named("high_done")
        low_done = sems.named("low_done")
        vectors_in = sems.named("vectors_in")
        values_spread = sems.named("values_spread")
        row_product = sems.named("row_product")
        row_done = sems.named("row_done")
        if rows is not None:
            value_columns, out_bias, row_tile = rows
            vcol = ctx.enter_context(nc.sbuf_tensor(f"{name}_vcol", [P, 4], F32))
            spread = ctx.enter_context(nc.sbuf_tensor(f"{name}_spread", [P, 4, P], F32))
            row_ps = ctx.enter_context(nc.psum_tensor(f"{name}_row_ps", [P, BANK], F32))
        block = ctx.enter_context(nc.Block())
        last = len(units) - 1

        @block.sync
        def _(sp):
            if rows is not None:
                for at, n, src in value_columns:
                    sp.dma_start(vcol[at:at + n, :], src, allow_slow_non_contiguous=True).then_inc(vectors_in, 16)
                sp.dma_start(row_tile[:, :], out_bias.partition_broadcast(P)).then_inc(vectors_in, 16)
            for i, (src, high, low) in enumerate(units):
                if i >= 3:
                    sp.wait_ge(high_done, i - 2)
                    sp.wait_ge(low_done, i - 2)
                k, n = src.shape[1], src.shape[2]
                sp.dma_start(stage[:, i % 3, 0:k, 0:n], src).then_inc(loaded[i % 3], 16)

        @block.scalar
        def _(act):
            for i, (src, high, low) in enumerate(units):
                k, n = src.shape[1], src.shape[2]
                act.wait_ge(loaded[i % 3], 16 * (i // 3 + 1))
                nc.scalar.copy(high, stage[:, i % 3, 0:k, 0:n]).then_inc(high_done, 1)

        @block.vector
        def _(dve):
            if rows is not None:
                dve.wait_ge(vectors_in, 16 * (len(value_columns) + 1))
                nc.vector.memset(spread[:, :, :], 1.0).then_inc(values_spread, 1)
                dve.wait_ge(values_spread, 1)
                for c in range(4):
                    nc.vector.tensor_scalar(spread[:, c, :], spread[:, c, :], vcol[:, c:c + 1], None,
                                            ALU.mult).then_inc(values_spread, 1)
            for i, (src, high, low) in enumerate(units):
                k, n = src.shape[1], src.shape[2]
                dve.wait_ge(high_done, i + 1)
                nc.vector.tensor_tensor(low, stage[:, i % 3, 0:k, 0:n], high.bitcast(F32),
                                        ALU.subtract).then_inc(low_done, 1)
            if rows is not None:
                dve.wait_ge(row_product, 1)
                nc.vector.tensor_tensor(rows[2][:, :], row_ps[:, :], rows[2][:, :],
                                        ALU.add).then_inc(row_done, 1)

        @block.tensor
        def _(pe):
            if rows is not None:
                pe.wait_ge(values_spread, 5)
                pe.wait_ge(loaded[last % 3], 16 * (last // 3 + 1))
                for c in range(4):
                    mm = nc.tensor.matmul(row_ps[:, :], spread[:, c, :], stage[:, last % 3, c, 0:BANK],
                                          start=c == 0, stop=c == 3)
                mm.then_inc(row_product, 1)


def project(nc, out, stationary, moving, chunks):
    for c in range(chunks):
        for n, (a, b) in enumerate(((1, 0), (0, 1), (0, 0))):
            mm = nc.tensor.matmul(out, stationary(c, a), moving(c, b),
                                  start=c == 0 and n == 0, stop=c == chunks - 1 and n == 2)
    return mm


def attention_phase(nc, sems, s, name, X, ident, minus_half, *, cross, grouped, eps, ctx_in, mask_in, mask_multiplies,
                    mask_per_sequence, weights, bias_q, bias_k, bias_v, bias_o, ln_s, ln_b,
                    scale, finish):
    wq, wk, wv, wo = weights
    D, C, G = s.D, s.C, s.G
    kd = wk.shape[1]
    KJ = kd // P
    HD = 16 if grouped else 32
    KVH = kd // HD
    U = GB * (D // HD) // UH
    UB = U // GB
    HDV = HD + 1

    if grouped:
        jobs = [("k", 0)] + [("q", m) for m in range(C)] + [("v", b) for b in range(GB)]
        before = {0: jobs[0:1], 1: jobs[2:3], 2: jobs[3:4], 3: jobs[4:5], 4: jobs[5:6]}
        after = {0: jobs[1:2], U - 1: jobs[6:7]}
    else:
        jobs = [("k", m) for m in range(KJ)] + [("q", m) for m in range(C)] + [("v", b) for b in range(GB)]
        before = {0: jobs[0:2], 1: jobs[4:6], 2: jobs[8:9]}
        after = {0: jobs[2:4], 1: jobs[6:8], U - 1: jobs[9:10]}
    job_bank = {job: 6 + j % 2 for j, job in enumerate(jobs)}
    job_before = {job: jobs[j - 2] if j >= 2 else None for j, job in enumerate(jobs)}

    with ExitStack() as ctx:
        def sb(n, shape, dt=F32):
            return ctx.enter_context(nc.sbuf_tensor(f"{name}_{n}", shape, dt))

        def sem(n):
            return sems.named(n)

        Wq = [sb(f"Wq{h}", [P, C, D], F32R) for h in "hl"]
        Wk = [sb(f"Wk{h}", [P, C, kd], F32R) for h in "hl"]
        Wv = [sb(f"Wv{h}", [P, C, kd], F32R) for h in "hl"]
        Wo = [sb(f"Wo{h}", [P, C, D], F32R) for h in "hl"]
        row_bias = sb("row_bias", [P, D])
        if grouped:
            by_head = bias_v.rearrange("(c a d) -> a d c", a=2, d=HD)
            value_columns = [(i * HD, HD, by_head[i // 4, :, :]) for i in range(P // HD)]
        else:
            value_columns = [(0, P, column(bias_v))]
        prepare_weights(nc, sems, name, [
            (weight(wq), Wq[0][:, :, :], Wq[1][:, :, :]),
            (weight(wk), Wk[0][:, :, :], Wk[1][:, :, :]),
            (weight(wv), Wv[0][:, :, :], Wv[1][:, :, :]),
            (weight(wo), Wo[0][:, :, :], Wo[1][:, :, :]),
        ], D, rows=(value_columns, bias_o, row_bias))

        xT = [sb(f"xT{h}", [P, C, TOK], F32R) for h in "hl"]
        cT = [sb(f"cT{h}", [P, C, TOK], F32R) for h in "hl"] if cross else xT
        zs = sb("zs", [P, GB, D])
        if not grouped:
            affine = sb("affine", [P, GB, C, P])
            ln_cols = sb("ln_cols", [P, 2, C])
        stats = sb("stats", [P, GB, 6])
        tick = sb("tick", [P, 2])
        mean_var = sb("mean_var", [P, GB, 4])
        ctx_rows = sb("ctx_rows", [P, GB, D]) if cross else None
        qT = sb("qT", [P, 2, C, TOK])
        if grouped:
            k_raw = sb("k_raw", [P, TOK])
            kT = sb("kT", [P, 2, C, GB, 2, P])
        else:
            kT = sb("kT", [P, 2, C, TOK])
        V = sb("V", [P, 2, GB, KVH, HDV])
        t = sb("t", [P, 4, 2, 4, P])
        pT = sb("pT", [P, 2, 4, P])
        neg_max = sb("neg_max", [P, 4, UH])
        recip = sb("recip", [P, 2, UH])
        o_rows = sb("o_rows", [P, GB, D])
        oT = [sb(f"oT{h}", [P, C, P], F32R) for h in "hl"]
        NM = 2 * GB if mask_per_sequence else 1
        mask = sb("mask", [P, NM, P])
        mask_add = sb("mask_add", [P, NM, P]) if mask_multiplies else None
        bq = sb("bq", [P, C])
        bk = sb("bk", [P, KJ])
        if finish:
            y = sb("y", [P, GB, D])
            fstats = sb("fstats", [P, GB, 6])
            fmv = sb("fmv", [P, GB, 4])
            gamma = sb("gamma", [P, D])
            beta = sb("beta", [P, D])

        score_ps = ctx.enter_context(nc.psum_tensor(f"{name}_scores", [P, 2, BANK], F32))
        other_ps = ctx.enter_context(nc.psum_tensor(f"{name}_others", [P, 6, BANK], F32))

        def bank(i):
            return other_ps[:, i - 2, :]

        def chunks(ap):
            return ap.rearrange("p (c k) -> p c k", k=P)

        small_in = sem("small_in")
        mask_loaded = [sem(f"mask_loaded{i}") for i in range(2)]
        ctx_loaded = sem("ctx_loaded")
        ones_set = sem("ones_set")
        rows_cleared = sem("rows_cleared")
        stats_done, aggr_done, eps_added, rstd_done, z_done = (
            sem(n) for n in ("stats_done", "aggr_done", "eps_added", "rstd_done", "z_done"))
        mask_ready = sem("mask_ready")
        row_added = sem("row_added")
        ctx_turned, x_turned = sem("ctx_turned"), sem("x_turned")
        c_high, c_low = sem("c_high"), sem("c_low")
        x_affine, x_high, x_low = sem("x_affine"), sem("x_high"), sem("x_low")
        made = {"k": sem("k_made"), "q": sem("q_made"), "v": sem("v_made")}
        kept = {"k": sem("k_kept"), "q": sem("q_kept"), "v": sem("v_kept")}
        per = {"k": KJ, "q": C, "v": GB}
        k_placed = sem("k_placed")
        scores_made, scores_read, mask_added, max_done, probs_done = (
            sem(n) for n in ("scores_made", "scores_read", "mask_added", "max_done", "probs_done"))
        probs_turned, pT_a, pT_b = sem("probs_turned"), sem("pT_a"), sem("pT_b")
        out_made, recip_done, out_kept = sem("out_made"), sem("recip_done"), sem("out_kept")
        out_turned, o_high, o_low = sem("out_turned"), sem("o_high"), sem("o_low")
        final_made, x_added = sem("final_made"), sem("x_added")
        if finish:
            f_stats, f_aggr, f_eps, f_rstd, f_z, f_scaled, f_shifted = (
                sem(n) for n in ("f_stats", "f_aggr", "f_eps", "f_rstd", "f_z", "f_scaled", "f_shifted"))
            stored = [sem(f"stored{i}") for i in range(GB)]

        PLACED = 16 * 32
        block = ctx.enter_context(nc.Block())

        def unit_heads(r, i):
            if not grouped:
                return i // 4, 2 * r + i // 4, i % 4, 0
            p, cc = r % 2, r // 2
            sl, c2, e = i // 4, (i // 2) % 2, i % 2
            return sl, 2 * p + sl, 2 * cc + c2, e

        def value_head(quadrant, c, e):
            return 2 * c + quadrant // 2 if grouped else 4 * c + quadrant

        def ahead(g, par, u):
            return (g, par, u + 2) if u + 2 < U else (g + 1, 1 - par, u + 2 - U)

        @block.sync
        def _(sp):
            if finish:
                for done in stored:
                    sp.sem_inc(done, 16)
            sp.sem_inc(k_placed, 16)
            sp.dma_start(bq[:, :], column(bias_q), allow_slow_non_contiguous=True).then_inc(small_in, 16)
            sp.dma_start(bk[:, :], column(bias_k), allow_slow_non_contiguous=True).then_inc(small_in, 16)
            if not grouped:
                sp.dma_start(ln_cols[:, 0, :], column(ln_s), allow_slow_non_contiguous=True).then_inc(small_in, 16)
                sp.dma_start(ln_cols[:, 1, :], column(ln_b), allow_slow_non_contiguous=True).then_inc(small_in, 16)
            if finish:
                sp.dma_start(gamma[:, :], finish[0].partition_broadcast(P)).then_inc(small_in, 16)
                sp.dma_start(beta[:, :], finish[1].partition_broadcast(P)).then_inc(small_in, 16)
            if not mask_per_sequence:
                sp.dma_start(mask[:, 0, :], mask_in[0, 0, :, :]).then_inc(mask_loaded[0], 16)

            def load_context(g):
                sp.wait_ge(ctx_turned, at(g * GB - 1))
                sp.dma_start(ctx_rows[:, :, :],
                             ctx_in[bass.ds(g * GB, GB), :, :].rearrange("b p d -> p b d")).then_inc(ctx_loaded, 16)

            def load_mask(g, par):
                sp.wait_ge(scores_read, at((g - 1) * U - 1))
                sp.dma_start(mask[:, par * GB:(par + 1) * GB, :], mask_in[bass.ds(g * GB, GB), 0, :, :].rearrange(
                    "b p k -> p b k")).then_inc(mask_loaded[par], 16)

            def place_keys(g, par):
                sp.wait_ge(kept["k"], at(g))
                sp.wait_ge(scores_made, at((g - 1) * U - 1))
                sp.wait_ge(rows_cleared, 1)
                for c in range(C):
                    for quadrant in range(4):
                        kv = 2 * c + quadrant // 2
                        for e in range(2):
                            row = QUAD * quadrant + HD * e
                            sp.dma_start(kT[row:row + HD, par, c, :, e, :],
                                         k_raw[HD * kv:HD * kv + HD, :].rearrange("p (b k) -> p b k", b=GB)
                                         ).then_inc(k_placed, 16)

            if mask_per_sequence:
                load_mask(0, 0)
            if cross:
                load_context(0)
            if grouped:
                place_keys(0, 0)
            if cross:
                load_context(1)

            def body(g, par, left):
                if mask_per_sequence and left >= 1:
                    load_mask(g + 1, 1 - par)
                if cross and left >= 2:
                    load_context(g + 2)
                if grouped and left >= 1:
                    place_keys(g + 1, 1 - par)
                if finish:
                    for b in range(GB):
                        sp.wait_ge(f_shifted, at(g * GB + b))
                        sp.dma_start(finish[3][bass.ds(g * GB + b, 1), :, :].rearrange("b p d -> p b d"),
                                     y[:, b:b + 1, :]).then_inc(stored[b], 16)

            if cross:
                over_groups(sp, G, body)
            if finish:
                for b in range(GB):
                    sp.wait_ge(stored[b], 16 * (G + 1))

        @block.gpsimd
        def _(pool):
            for done in (rstd_done, row_added, mask_added):
                pool.sem_inc(done, AHEAD)
            if finish:
                for done in (f_rstd, f_scaled, f_shifted):
                    pool.sem_inc(done, AHEAD)
            if grouped:
                nc.gpsimd.memset(kT[:, :, :, :, :, :].rearrange("p a c b e k -> p (a c b e k)"),
                                 0.0).then_inc(rows_cleared, 1)

            def root(g):
                pool.wait_ge(eps_added, at(g))
                nc.gpsimd.tensor_tensor(mean_var[:, :, 3], mean_var[:, :, 2], minus_half[:, 0:GB],
                                        ALU.pow).then_inc(rstd_done, 1)

            def add_row_bias(g):
                for b in range(GB):
                    pool.wait_ge(z_done, at(g * GB + b))
                    xb = X[:, bass.ds(g * GB + b, 1), :].rearrange("p b d -> p (b d)")
                    nc.gpsimd.tensor_tensor(xb, xb, row_bias[:, :], ALU.add).then_inc(row_added, 1)

            def add_mask(g, par, u):
                n = g * U + u
                pool.wait_ge(scores_read, at(n))
                if u == 0:
                    pool.wait_ge(mask_ready, at(g if mask_per_sequence else 0))
                m = par * GB + u // UB if mask_per_sequence else 0
                tu = t[:, u % 4, :, :, :].rearrange("p a c k -> p (a c) k")
                nc.gpsimd.tensor_tensor(tu, tu, mask_add[:, m:m + 1, :].to_broadcast([P, UH, P]),
                                        ALU.add).then_inc(mask_added, 1)

            def finish_row(g, b):
                pool.wait_ge(f_eps, at(g * GB + b))
                nc.gpsimd.tensor_tensor(fmv[:, b, 3:4], fmv[:, b, 2:3], minus_half[:, 0:1],
                                        ALU.pow).then_inc(f_rstd, 1)
                pool.wait_ge(f_z, at(g * GB + b))
                yb = y[:, b, :]
                nc.gpsimd.tensor_tensor(yb, yb, gamma[:, :], ALU.mult).then_inc(f_scaled, 1)
                pool.wait_ge(f_scaled, at(g * GB + b))
                nc.gpsimd.tensor_tensor(yb, yb, beta[:, :], ALU.add).then_inc(f_shifted, 1)

            if finish:
                pool.wait_ge(small_in, 16 * 4)
            for g in range(2):
                if not grouped:
                    root(g)
                add_row_bias(g)
            if mask_multiplies:
                add_mask(0, 0, 0)
                add_mask(0, 0, 1)

            def body(g, par, left):
                for u in range(U):
                    if mask_multiplies and (left or u + 2 < U):
                        add_mask(*ahead(g, par, u))
                    if u == UB + 1 and finish:
                        finish_row(g, 0)
                    if u == U - 2 and not grouped and left >= 2:
                        root(g + 2)
                if left >= 2:
                    add_row_bias(g + 2)
                if finish:
                    finish_row(g, 1)

            over_groups(pool, G, body)

        @block.scalar
        def _(act):
            for done in (c_high, x_affine, kept["k"], kept["v"], probs_done, pT_a, o_high):
                act.sem_inc(done, AHEAD)
            if grouped:
                act.sem_inc(x_high, AHEAD)
            act.wait_ge(small_in, 16 * 4)
            act.wait_ge(ones_set, 1)

            def transposed_high(g):
                if cross:
                    for b in range(GB):
                        act.wait_ge(ctx_turned, at(g * GB + b))
                        if b == 0:
                            act.wait_ge(made["v"], at(g * GB - 1))
                        nc.scalar.copy(cT[0][:, :, b * P:(b + 1) * P], chunks(bank(6 + b))).then_inc(c_high, 1)
                for b in range(GB):
                    act.wait_ge(x_turned, at(g * GB + b))
                    if grouped:
                        if b == 0:
                            act.wait_ge(made["q"], at(g * C - 1))
                        nc.scalar.copy(xT[0][:, :, b * P:(b + 1) * P], chunks(bank(6 + b))).then_inc(x_high, 1)
                    else:
                        act.wait_ge(x_low, at((g - 1) * GB + b))
                        for c in range(C):
                            ins = nc.scalar.activation(
                                affine[:, b, c, :], bank(6 + b)[:, c * P:(c + 1) * P], ACT.Identity,
                                bias=ln_cols[:, 1, c:c + 1], scale=ln_cols[:, 0, c:c + 1])
                        ins.then_inc(x_affine, 1)

            def keep(g, par, job):
                kind, m = job
                if kind == "q":
                    return
                act.wait_ge(made[kind], at(g * per[kind] + m))
                src = bank(job_bank[job])
                if kind == "k":
                    if m == 0:
                        act.wait_ge(scores_made, at((g - 1) * U - 1))
                        if grouped:
                            act.wait_ge(k_placed, PLACED * g + 16)
                    dst = k_raw[:, :] if grouped else kT[:, par, m, :]
                    nc.scalar.activation(dst, src[:, 0:TOK], ACT.Identity, bias=bk[:, m:m + 1]).then_inc(kept["k"], 1)
                else:
                    if m == 0:
                        act.wait_ge(out_made, at((g - 1) * U - 1))
                    nc.scalar.copy(V[:, par, m, :, 0:HD],
                                   src[:, 0:kd].rearrange("p (h d) -> p h d", h=KVH)).then_inc(kept["v"], 1)

            def probabilities(g, par, u):
                act.wait_ge(max_done, at(g * U + u))
                tu = t[:, u % 4, :, :, :].rearrange("p a c k -> p (a c) k")
                for i in range(UH):
                    ins = nc.scalar.activation(tu[:, i, :], tu[:, i, :], ACT.Exp, bias=neg_max[:, u % 4, i:i + 1])
                    if i % 4 == 3:
                        ins.then_inc(probs_done, 1)

            def output_high(n):
                act.wait_ge(out_turned, at(n))
                act.wait_ge(final_made, at(n - 1))
                nc.scalar.copy(oT[0][:, :, :], chunks(bank(5))).then_inc(o_high, 1)

            transposed_high(0)
            for job in jobs:
                keep(0, 0, job)
            transposed_high(1)
            probabilities(0, 0, 0)
            probabilities(0, 0, 1)

            def body(g, par, left):
                for u in range(U):
                    n = g * U + u
                    act.wait_ge(probs_turned, at(2 * n))
                    act.wait_ge(out_made, at(n - 1))
                    nc.scalar.copy(pT[:, 0, :, :], chunks(bank(2))).then_inc(pT_a, 1)
                    if u == UB:
                        output_high(g * GB)
                    if left:
                        for job in before.get(u, ()):
                            keep(g + 1, 1 - par, job)
                    if left or u + 2 < U:
                        probabilities(*ahead(g, par, u))
                    if left:
                        for job in after.get(u, ()):
                            keep(g + 1, 1 - par, job)
                output_high(g * GB + 1)
                if left >= 2:
                    transposed_high(g + 2)

            over_groups(act, G, body)

        @block.vector
        def _(dve):
            for done in (c_low, x_low, kept["q"], scores_read, max_done, pT_b, out_kept, o_low, x_added, z_done,
                         stats_done, aggr_done, eps_added, mask_ready, recip_done):
                dve.sem_inc(done, AHEAD)
            if not grouped:
                dve.sem_inc(x_high, AHEAD)
            if finish:
                for done in (f_stats, f_aggr, f_eps, f_z):
                    dve.sem_inc(done, AHEAD)
            nc.vector.memset(V[:, :, :, :, HD:HDV].rearrange("p a b h o -> p (a b h) o"), 1.0).then_inc(ones_set, 1)
            dve.wait_ge(small_in, 16 * 4)

            def x_row(g, b):
                return X[:, bass.ds(g * GB + b, 1), :].rearrange("p b d -> p (b d)")

            def normalise(g):
                dve.wait_ge(x_turned, at(g * GB - 1))
                if grouped:
                    for b in range(GB):
                        nc.vector.tensor_copy(zs[:, b, :], x_row(g, b)).then_inc(z_done, 1)
                    return
                for b in range(GB):
                    nc.vector.bn_stats(stats[:, b, :], x_row(g, b)).then_inc(stats_done, 1)
                dve.wait_ge(stats_done, at(g * GB + GB - 1))
                nc.vector.memset(tick[:, 0:1], 0.0)
                for b in range(GB):
                    nc.vector.bn_aggr(mean_var[:, b, 0:2], stats[:, b, :]).then_inc(aggr_done, 1)
                dve.wait_ge(aggr_done, at(g * GB + GB - 1))
                nc.vector.tensor_scalar(mean_var[:, :, 2], mean_var[:, :, 1], eps, None,
                                        ALU.add).then_inc(eps_added, 1)
                dve.wait_ge(rstd_done, at(g))
                for b in range(GB):
                    nc.vector.tensor_scalar(zs[:, b, :], x_row(g, b), mean_var[:, b, 0:1], mean_var[:, b, 3:4],
                                            ALU.subtract, ALU.mult).then_inc(z_done, 1)

            def context_low(g):
                if not cross:
                    return
                for b in range(GB):
                    dve.wait_ge(c_high, at(g * GB + b))
                    tok = slice(b * P, (b + 1) * P)
                    nc.vector.tensor_tensor(cT[1][:, :, tok], chunks(bank(6 + b)),
                                            cT[0][:, :, tok].bitcast(F32), ALU.subtract).then_inc(c_low, 1)

            def x_halves(g):
                for b in range(GB):
                    tok = slice(b * P, (b + 1) * P)
                    if grouped:
                        dve.wait_ge(x_high, at(g * GB + b))
                        nc.vector.tensor_tensor(xT[1][:, :, tok], chunks(bank(6 + b)),
                                                xT[0][:, :, tok].bitcast(F32), ALU.subtract).then_inc(x_low, 1)
                        continue
                    dve.wait_ge(x_affine, at(g * GB + b))
                    if b == 0:
                        dve.wait_ge(made["q"], at(g * C - 1))
                        if not cross:
                            dve.wait_ge(made["v"], at(g * GB - 1))
                    nc.vector.tensor_copy(xT[0][:, :, tok], affine[:, b, :, :]).then_inc(x_high, 1)
                    dve.wait_ge(x_high, at(g * GB + b))
                    nc.vector.tensor_tensor(xT[1][:, :, tok], affine[:, b, :, :],
                                            xT[0][:, :, tok].bitcast(F32), ALU.subtract).then_inc(x_low, 1)

            def keep_queries(g, par, job):
                kind, m = job
                if kind != "q":
                    return
                dve.wait_ge(made["q"], at(g * C + m))
                if m == 0:
                    dve.wait_ge(scores_made, at((g - 1) * U - 1))
                nc.vector.tensor_scalar(qT[:, par, m, :], bank(job_bank[job])[:, 0:TOK], bq[:, m:m + 1], scale,
                                        ALU.add, ALU.mult).then_inc(kept["q"], 1)

            def prepare_mask(g, par):
                if mask_multiplies and mask_per_sequence:
                    dve.wait_ge(mask_loaded[par], 8 * (g - par) + 16)
                    dve.wait_ge(mask_added, at((g - 1) * U - 1))
                    m = slice(par * GB, (par + 1) * GB)
                    nc.vector.tensor_scalar(mask_add[:, m, :], mask[:, m, :], 1.0, 10000.0,
                                            ALU.subtract, ALU.mult).then_inc(mask_ready, 1)

            def read_scores(g, par, u):
                n = g * U + u
                dve.wait_ge(scores_made, at(n))
                dve.wait_ge(probs_turned, at(2 * (n - 4) + 1))
                m = 0
                if mask_per_sequence:
                    m = par * GB + u // UB
                    if u == 0:
                        dve.wait_ge(mask_loaded[par], 8 * (g - par) + 16)
                sc = score_ps[:, :, :].rearrange("p a (c k) -> p (a c) k", k=P)
                tu = t[:, u % 4, :, :, :].rearrange("p a c k -> p (a c) k")
                nc.vector.tensor_tensor(tu, sc, mask[:, m:m + 1, :].to_broadcast([P, UH, P]),
                                        ALU.mult if mask_multiplies else ALU.add).then_inc(scores_read, 1)

            def row_max(g, par, u):
                n = g * U + u
                dve.wait_ge(mask_added if mask_multiplies else scores_read, at(n))
                tu = t[:, u % 4, :, :, :].rearrange("p a c k -> p (a c) k")
                nc.vector.tensor_reduce(neg_max[:, u % 4, :], tu, AX.X, ALU.max, negate=True).then_inc(max_done, 1)

            def keep_output(g, u):
                b, r = u // UB, u % UB
                n = g * U + u
                dve.wait_ge(out_made, at(n))
                o = bank(4)[:, 0:UH * HDV].rearrange("p (i d) -> p i d", i=UH)
                nc.vector.reciprocal(recip[:, u % 2, :], o[:, :, HD]).then_inc(recip_done, 1)
                dve.wait_ge(recip_done, at(n))
                if r == 0:
                    dve.wait_ge(out_turned, at((g - 1) * GB + b))
                if not grouped:
                    dst = o_rows[:, b, :].rearrange("p (c j d) -> p j c d", c=C, j=4)[:, 2 * r:2 * r + 2, :, :]
                    rec = recip[:, u % 2, :].rearrange("p (a c) -> p a c", a=2).unsqueeze(3)
                    ins = nc.vector.tensor_tensor(dst, o[:, :, 0:HD].rearrange("p (a c) d -> p a c d", a=2),
                                                  rec.to_broadcast([P, 2, C, HD]), ALU.mult)
                else:
                    p, cc = r % 2, r // 2
                    for sl in range(2):
                        dst = o_rows[:, b, :].rearrange("p (c j e d) -> p c j e d", c=C, j=4, e=2)[
                            :, 2 * cc:2 * cc + 2, 2 * p + sl, :, :]
                        src = o[:, 4 * sl:4 * sl + 4, 0:HD].rearrange("p (c e) d -> p c e d", c=2)
                        rec = recip[:, u % 2, 4 * sl:4 * sl + 4].rearrange("p (c e) -> p c e", c=2).unsqueeze(3)
                        ins = nc.vector.tensor_tensor(dst, src, rec.to_broadcast([P, 2, 2, HD]), ALU.mult)
                ins.then_inc(out_kept, 1)

            def output_low(n):
                dve.wait_ge(o_high, at(n))
                nc.vector.tensor_tensor(oT[1][:, :, :], chunks(bank(5)), oT[0][:, :, :].bitcast(F32),
                                        ALU.subtract).then_inc(o_low, 1)

            def add_output(g, b):
                n = g * GB + b
                dve.wait_ge(final_made, at(n))
                dve.wait_ge(row_added, at(n))
                if not finish:
                    nc.vector.tensor_tensor(x_row(g, b), bank(5), x_row(g, b), ALU.add).then_inc(x_added, 1)
                    return
                yb = y[:, b, :]
                dve.wait_ge(stored[b], 16 * g + 16)
                nc.vector.tensor_tensor(yb, bank(5), x_row(g, b), ALU.add).then_inc(x_added, 1)
                dve.wait_ge(x_added, at(n))
                nc.vector.bn_stats(fstats[:, b, :], yb).then_inc(f_stats, 1)
                dve.wait_ge(f_stats, at(n))
                nc.vector.memset(tick[:, b:b + 1], 0.0)
                nc.vector.bn_aggr(fmv[:, b, 0:2], fstats[:, b, :]).then_inc(f_aggr, 1)
                dve.wait_ge(f_aggr, at(n))
                nc.vector.tensor_scalar(fmv[:, b, 2:3], fmv[:, b, 1:2], finish[2], None, ALU.add).then_inc(f_eps, 1)

            def finish_row(g, b):
                if finish:
                    dve.wait_ge(f_rstd, at(g * GB + b))
                    yb = y[:, b, :]
                    nc.vector.tensor_scalar(yb, yb, fmv[:, b, 0:1], fmv[:, b, 3:4], ALU.subtract,
                                            ALU.mult).then_inc(f_z, 1)

            normalise(0)
            context_low(0)
            x_halves(0)
            normalise(1)
            if mask_multiplies and not mask_per_sequence:
                dve.wait_ge(mask_loaded[0], 16)
                nc.vector.tensor_scalar(mask_add[:, :, :], mask[:, :, :], 1.0, 10000.0,
                                        ALU.subtract, ALU.mult).then_inc(mask_ready, 1)
            prepare_mask(0, 0)
            for job in jobs:
                keep_queries(0, 0, job)
            read_scores(0, 0, 0)
            context_low(1)
            x_halves(1)
            read_scores(0, 0, 1)
            row_max(0, 0, 0)
            row_max(0, 0, 1)

            def body(g, par, left):
                for u in range(U):
                    n = g * U + u
                    more = left or u + 2 < U
                    dve.wait_ge(probs_turned, at(2 * n + 1))
                    dve.wait_ge(out_made, at(n - 1))
                    nc.vector.tensor_copy(pT[:, 1, :, :], chunks(bank(3))).then_inc(pT_b, 1)
                    if more:
                        read_scores(*ahead(g, par, u))
                    if more and not mask_multiplies:
                        row_max(*ahead(g, par, u))
                    if u == 0 and left:
                        prepare_mask(g + 1, 1 - par)
                    if u == UB:
                        output_low(g * GB)
                    if left:
                        for job in before.get(u, ()):
                            keep_queries(g + 1, 1 - par, job)
                    keep_output(g, u)
                    if more and mask_multiplies:
                        row_max(*ahead(g, par, u))
                    if u == UB:
                        add_output(g, 0)
                    if u == min(UB + 1, U - 1):
                        finish_row(g, 0)
                    if left:
                        for job in after.get(u, ()):
                            keep_queries(g + 1, 1 - par, job)
                    if u == U - 2 and left >= 2:
                        normalise(g + 2)
                output_low(g * GB + 1)
                if left >= 2:
                    context_low(g + 2)
                    x_halves(g + 2)
                add_output(g, 1)
                finish_row(g, 1)

            over_groups(dve, G, body)

        @block.tensor
        def _(pe):
            for done in (ctx_turned, x_turned, made["k"], made["q"], made["v"], scores_made, probs_turned, out_made,
                         out_turned, final_made):
                pe.sem_inc(done, AHEAD)
            pe.wait_ge(ones_set, 1)

            def turn_rows(g):
                pe.wait_ge(kept["v"], at(g * GB - 1))
                if cross:
                    pe.wait_ge(ctx_loaded, 16 * g + 16)
                    for b in range(GB):
                        for c in range(C):
                            mm = nc.tensor.transpose(bank(6 + b)[:, c * P:(c + 1) * P],
                                                     ctx_rows[:, b, c * P:(c + 1) * P], ident[:, :])
                        mm.then_inc(ctx_turned, 1)
                for b in range(GB):
                    pe.wait_ge(z_done, at(g * GB + b))
                    if cross:
                        pe.wait_ge(c_low, at(g * GB + b))
                    for c in range(C):
                        mm = nc.tensor.transpose(bank(6 + b)[:, c * P:(c + 1) * P], zs[:, b, c * P:(c + 1) * P],
                                                 ident[:, :])
                    mm.then_inc(x_turned, 1)

            def make(g, par, job):
                kind, m = job
                out = bank(job_bank[job])
                prev = job_before[job]
                if prev:
                    pe.wait_ge(kept[prev[0]], at(g * per[prev[0]] + prev[1]))
                elif not grouped:
                    pe.wait_ge(x_affine, at(g * GB + job_bank[job] - 6))
                if (kind == "k" and m == 0 and cross):
                    pe.wait_ge(c_low, at(g * GB + GB - 1))
                    if grouped:
                        pe.wait_ge(x_low, at(g * GB + GB - 1))
                elif m == 0:
                    pe.wait_ge(x_low, at(g * GB + GB - 1))
                if kind == "k":
                    mm = project(nc, out[:, 0:TOK], lambda c, h: Wk[h][:, c, m * P:(m + 1) * P],
                                 lambda c, h: cT[h][:, c, :], C)
                elif kind == "q":
                    mm = project(nc, out[:, 0:TOK], lambda c, h: Wq[h][:, c, m * P:(m + 1) * P],
                                 lambda c, h: xT[h][:, c, :], C)
                else:
                    mm = project(nc, out[:, 0:kd], lambda c, h: cT[h][:, c, m * P:(m + 1) * P],
                                 lambda c, h: Wv[h][:, c, :], C)
                mm.then_inc(made[kind], 1)

            def scores(g, par, u):
                b, r = u // UB, u % UB
                pe.wait_ge(scores_read, at(g * U + u - 1))
                if u == 0:
                    pe.wait_ge(kept["q"], at(g * C + C - 1))
                    if grouped:
                        pe.wait_ge(k_placed, PLACED * g + PLACED + 16)
                    else:
                        pe.wait_ge(kept["k"], at(g * KJ + KJ - 1))
                tok = slice(b * P, (b + 1) * P)
                for i in (0, 4, 1, 5, 2, 6, 3, 7):
                    sl, q, c, e = unit_heads(r, i)
                    rows = slice(QUAD * q, QUAD * q + QUAD)
                    if not grouped:
                        mm = nc.tensor.matmul(score_ps[:, sl, c * P:(c + 1) * P], qT[rows, par, c, tok],
                                              kT[rows, par, c, tok], start=True, stop=True)
                    elif e == 0:
                        col = (i // 2) % 2 * 2 * P
                        mm = nc.tensor.matmul(score_ps[:, sl, col:col + 2 * P], qT[rows, par, c, tok],
                                              kT[rows, par, c, b, :, :].rearrange("p e k -> p (e k)"),
                                              start=True, stop=True)
                mm.then_inc(scores_made, 1)

            def turn_probs(n, u):
                for sl in range(2):
                    pe.wait_ge(probs_done, at(2 * n + sl))
                    pe.wait_ge(pT_b if sl else pT_a, at(n - 1))
                    for c in range(4):
                        mm = nc.tensor.transpose(bank(2 + sl)[:, c * P:(c + 1) * P], t[:, u % 4, sl, c, :],
                                                 ident[:, :])
                    mm.then_inc(probs_turned, 1)

            def outputs(g, par, u):
                n = g * U + u
                b, r = u // UB, u % UB
                pe.wait_ge(pT_a, at(n))
                pe.wait_ge(out_kept, at(n - 1))
                if u == 0:
                    pe.wait_ge(kept["v"], at(g * GB + GB - 1))
                for i in range(UH):
                    if i == 4:
                        pe.wait_ge(pT_b, at(n))
                    sl, q, c, e = unit_heads(r, i)
                    mm = nc.tensor.matmul(bank(4)[:, i * HDV:(i + 1) * HDV], pT[:, sl, i % 4, :],
                                          V[:, par, b, value_head(q, c, e), :], start=True, stop=True)
                mm.then_inc(out_made, 1)

            def turn_output(g, b):
                pe.wait_ge(out_kept, at(g * U + (b + 1) * UB - 1))
                pe.wait_ge(x_added, at(g * GB + b - 1))
                for c in range(C):
                    mm = nc.tensor.transpose(bank(5)[:, c * P:(c + 1) * P], o_rows[:, b, c * P:(c + 1) * P],
                                             ident[:, :])
                mm.then_inc(out_turned, 1)

            def project_output(n):
                pe.wait_ge(o_low, at(n))
                project(nc, bank(5), lambda c, h: oT[h][:, c, :], lambda c, h: Wo[h][:, c, :],
                        C).then_inc(final_made, 1)

            turn_rows(0)
            for job in jobs:
                make(0, 0, job)
            scores(0, 0, 0)
            turn_rows(1)
            scores(0, 0, 1)

            def body(g, par, left):
                for u in range(U):
                    turn_probs(g * U + u, u)
                    if left or u + 2 < U:
                        scores(*ahead(g, par, u))
                    if u == UB:
                        turn_output(g, 0)
                    if left:
                        for job in before.get(u, ()):
                            make(g + 1, 1 - par, job)
                    outputs(g, par, u)
                    if u == UB:
                        project_output(g * GB)
                    if left:
                        for job in after.get(u, ()):
                            make(g + 1, 1 - par, job)
                turn_output(g, 1)
                if left >= 2:
                    turn_rows(g + 2)
                project_output(g * GB + 1)

            over_groups(pe, G, body)


def mlp_phase(nc, sems, s, X, ident, minus_half, *, eps, w1, b1, w2, b2, ln_s, ln_b):
    D, C, G, M = s.D, s.C, s.G, s.M
    A_AT = M // 2
    with ExitStack() as ctx:
        def sb(n, shape, dt=F32):
            return ctx.enter_context(nc.sbuf_tensor(f"mlp_{n}", shape, dt))

        def sem(n):
            return sems.named(n)

        W1 = [sb(f"W1{h}", [P, C, s.F], F32R) for h in "hl"]
        W2 = [sb(f"W2{h}", [P, M, D], F32R) for h in "hl"]
        w2v = weight(w2)
        prepare_weights(nc, sems, "mlp", [
            (weight(w1)[:, :, n:n + D], W1[0][:, :, n:n + D], W1[1][:, :, n:n + D]) for n in range(0, s.F, D)
        ] + [(w2v[:, k:k + 4, :], W2[0][:, k:k + 4, :], W2[1][:, k:k + 4, :]) for k in range(0, M, 4)], D)

        xT = [sb(f"xT{h}", [P, 2, C, TOK], F32R) for h in "hl"]
        zs = sb("zs", [P, GB, D])
        affine = sb("affine", [P, GB, C, P])
        ln_cols = sb("ln_cols", [P, 2, C])
        b1_cols = sb("b1_cols", [P, M])
        row_bias = sb("row_bias", [P, D])
        stats = sb("stats", [P, GB, 6])
        tick = sb("tick", [P, 2])
        mean_var = sb("mean_var", [P, GB, 4])
        hidden = sb("hidden", [P, 4, TOK])
        hT = [sb(f"hT{h}", [P, 4, TOK], F32R) for h in "hl"]
        sums = ctx.enter_context(nc.psum_tensor("mlp_sums", [P, GB, BANK], F32))
        turned = ctx.enter_context(nc.psum_tensor("mlp_turned", [P, GB, BANK], F32))
        work = ctx.enter_context(nc.psum_tensor("mlp_work", [P, 4, BANK], F32))

        small_in = sem("small_in")
        stats_done, aggr_done, eps_added, rstd_done, z_done = (
            sem(n) for n in ("stats_done", "aggr_done", "eps_added", "rstd_done", "z_done"))
        row_added, x_turned, x_affine, x_high, x_low = (
            sem(n) for n in ("row_added", "x_turned", "x_affine", "x_high", "x_low"))
        hidden_made, gelu_done, h_high, h_low, chunk_used, x_added = (
            sem(n) for n in ("hidden_made", "gelu_done", "h_high", "h_low", "chunk_used", "x_added"))
        block = ctx.enter_context(nc.Block())

        def ahead(g, par, m):
            return (g, par, m + 2) if m + 2 < M else (g + 1, 1 - par, m + 2 - M)

        @block.sync
        def _(sp):
            sp.dma_start(ln_cols[:, 0, :], column(ln_s), allow_slow_non_contiguous=True).then_inc(small_in, 16)
            sp.dma_start(ln_cols[:, 1, :], column(ln_b), allow_slow_non_contiguous=True).then_inc(small_in, 16)
            sp.dma_start(b1_cols[:, :], column(b1), allow_slow_non_contiguous=True).then_inc(small_in, 16)
            sp.dma_start(row_bias[:, :], b2.partition_broadcast(P)).then_inc(small_in, 16)

        @block.gpsimd
        def _(pool):
            for done in (rstd_done, row_added):
                pool.sem_inc(done, AHEAD)
            pool.wait_ge(small_in, 16 * 4)

            def side(g):
                pool.wait_ge(eps_added, at(g))
                nc.gpsimd.tensor_tensor(mean_var[:, :, 3], mean_var[:, :, 2], minus_half[:, 0:GB],
                                        ALU.pow).then_inc(rstd_done, 1)
                for b in range(GB):
                    pool.wait_ge(z_done, at(g * GB + b))
                    xb = X[:, bass.ds(g * GB + b, 1), :].rearrange("p b d -> p (b d)")
                    nc.gpsimd.tensor_tensor(xb, xb, row_bias[:, :], ALU.add).then_inc(row_added, 1)

            side(0)

            def body(g, par, left):
                if left:
                    side(g + 1)

            over_groups(pool, G, body)

        @block.scalar
        def _(act):
            for done in (gelu_done, x_affine):
                act.sem_inc(done, AHEAD)
            act.wait_ge(small_in, 16 * 4)

            def affine_rows(g):
                for b in range(GB):
                    act.wait_ge(x_turned, at(g * GB + b))
                    act.wait_ge(x_low, at((g - 1) * GB + b))
                    for c in range(C):
                        ins = nc.scalar.activation(affine[:, b, c, :], turned[:, b, c * P:(c + 1) * P], ACT.Identity,
                                                   bias=ln_cols[:, 1, c:c + 1], scale=ln_cols[:, 0, c:c + 1])
                    ins.then_inc(x_affine, 1)

            def gelu(g, par, m):
                n = g * M + m
                act.wait_ge(hidden_made, at(n))
                act.wait_ge(h_low, at(n - 4))
                nc.scalar.activation(hidden[:, m % 4, :], work[:, m % 4, 0:TOK], ACT.Gelu_apprx_tanh,
                                     bias=b1_cols[:, m:m + 1]).then_inc(gelu_done, 1)

            affine_rows(0)
            gelu(0, 0, 0)
            gelu(0, 0, 1)

            def body(g, par, left):
                for m in range(M):
                    if left or m + 2 < M:
                        gelu(*ahead(g, par, m))
                    if m == A_AT and left:
                        affine_rows(g + 1)

            over_groups(act, G, body)

        @block.vector
        def _(dve):
            for done in (x_low, x_high, x_added, z_done, stats_done, aggr_done, eps_added, h_high, h_low):
                dve.sem_inc(done, AHEAD)

            def x_row(g, b):
                return X[:, bass.ds(g * GB + b, 1), :].rearrange("p b d -> p (b d)")

            def normalise(g):
                dve.wait_ge(x_turned, at(g * GB - 1))
                for b in range(GB):
                    nc.vector.bn_stats(stats[:, b, :], x_row(g, b)).then_inc(stats_done, 1)
                dve.wait_ge(stats_done, at(g * GB + GB - 1))
                nc.vector.memset(tick[:, 0:1], 0.0)
                for b in range(GB):
                    nc.vector.bn_aggr(mean_var[:, b, 0:2], stats[:, b, :]).then_inc(aggr_done, 1)
                dve.wait_ge(aggr_done, at(g * GB + GB - 1))
                nc.vector.tensor_scalar(mean_var[:, :, 2], mean_var[:, :, 1], eps, None,
                                        ALU.add).then_inc(eps_added, 1)
                dve.wait_ge(rstd_done, at(g))
                for b in range(GB):
                    nc.vector.tensor_scalar(zs[:, b, :], x_row(g, b), mean_var[:, b, 0:1], mean_var[:, b, 3:4],
                                            ALU.subtract, ALU.mult).then_inc(z_done, 1)

            def x_halves(g, par):
                dve.wait_ge(hidden_made, at((g - 1) * M - 1))
                for b in range(GB):
                    tok = slice(b * P, (b + 1) * P)
                    dve.wait_ge(x_affine, at(g * GB + b))
                    nc.vector.tensor_copy(xT[0][:, par, :, tok], affine[:, b, :, :]).then_inc(x_high, 1)
                    dve.wait_ge(x_high, at(g * GB + b))
                    nc.vector.tensor_tensor(xT[1][:, par, :, tok], affine[:, b, :, :],
                                            xT[0][:, par, :, tok].bitcast(F32), ALU.subtract).then_inc(x_low, 1)

            def hidden_halves(g, par, m):
                n = g * M + m
                dve.wait_ge(gelu_done, at(n))
                dve.wait_ge(chunk_used, at(n - 4))
                nc.vector.tensor_copy(hT[0][:, m % 4, :], hidden[:, m % 4, :]).then_inc(h_high, 1)
                dve.wait_ge(h_high, at(n))
                nc.vector.tensor_tensor(hT[1][:, m % 4, :], hidden[:, m % 4, :],
                                        hT[0][:, m % 4, :].bitcast(F32), ALU.subtract).then_inc(h_low, 1)

            normalise(0)
            x_halves(0, 0)
            hidden_halves(0, 0, 0)
            hidden_halves(0, 0, 1)

            def body(g, par, left):
                for m in range(M):
                    if left or m + 2 < M:
                        hidden_halves(*ahead(g, par, m))
                    if left and m == A_AT - 2:
                        normalise(g + 1)
                    if left and m == A_AT:
                        x_halves(g + 1, 1 - par)
                for b in range(GB):
                    dve.wait_ge(row_added, at(g * GB + b))
                    dve.wait_ge(chunk_used, at(g * M + M - 1))
                    nc.vector.tensor_tensor(x_row(g, b), sums[:, b, :], x_row(g, b), ALU.add).then_inc(x_added, 1)

            over_groups(dve, G, body)

        @block.tensor
        def _(pe):
            for done in (x_turned, chunk_used, hidden_made):
                pe.sem_inc(done, AHEAD)

            def turn_rows(g):
                for b in range(GB):
                    pe.wait_ge(z_done, at(g * GB + b))
                    pe.wait_ge(x_affine, at((g - 1) * GB + b))
                    for c in range(C):
                        mm = nc.tensor.transpose(turned[:, b, c * P:(c + 1) * P], zs[:, b, c * P:(c + 1) * P],
                                                 ident[:, :])
                    mm.then_inc(x_turned, 1)

            def hidden_chunk(g, par, m):
                n = g * M + m
                if m == 0:
                    pe.wait_ge(x_low, at(g * GB + GB - 1))
                pe.wait_ge(gelu_done, at(n - 4))
                project(nc, work[:, m % 4, 0:TOK], lambda c, h: W1[h][:, c, m * P:(m + 1) * P],
                        lambda c, h: xT[h][:, par, c, :], C).then_inc(hidden_made, 1)

            turn_rows(0)
            hidden_chunk(0, 0, 0)
            hidden_chunk(0, 0, 1)

            def body(g, par, left):
                for m in range(M):
                    n = g * M + m
                    pe.wait_ge(h_low, at(n))
                    if m == 0:
                        pe.wait_ge(x_added, at(g * GB - 1))
                    for b in range(GB):
                        tok = slice(b * P, (b + 1) * P)
                        for k, (ha, hb) in enumerate(((1, 0), (0, 1), (0, 0))):
                            mm = nc.tensor.matmul(sums[:, b, :], hT[ha][:, m % 4, tok], W2[hb][:, m, :],
                                                  start=m == 0 and k == 0, stop=m == M - 1 and k == 2)
                    mm.then_inc(chunk_used, 1)
                    if left or m + 2 < M:
                        hidden_chunk(*ahead(g, par, m))
                    if left and m == A_AT:
                        turn_rows(g + 1)

            over_groups(pe, G, body)


def load_residual(nc, sems, s, x, X, ident, minus_half):
    with ExitStack() as ctx:
        x_in = sems.named("x_in")
        set_up = sems.named("set_up")
        block = ctx.enter_context(nc.Block())

        @block.sync
        def _(sp):
            for b in range(0, s.NB, 4):
                sp.dma_start(X[:, b:b + 4, :], x[b:b + 4, :, :].rearrange("b p d -> p b d")).then_inc(x_in, 16)
            sp.wait_ge(x_in, 16 * (s.NB // 4))

        @block.gpsimd
        def _(pool):
            nc.gpsimd.memset(ident[:, :], 0.0).then_inc(set_up, 1)
            nc.gpsimd.memset(minus_half[:, :], -0.5).then_inc(set_up, 1)
            pool.wait_ge(set_up, 2)
            nc.gpsimd.affine_select(out=ident[:, :], in_=ident[:, :], compare_op=ALU.not_equal, fill=1.0, base=0,
                                    pattern=[[-1, P]], channel_multiplier=1).then_inc(set_up, 1)
            pool.wait_ge(set_up, 3)


def build_cross_attention_layers(nc, a, out):
    s = Shape(a["x"], a["L0_xattn_w1"])
    D = s.D
    with ExitStack() as ctx:
        sems = Semaphores(nc, ctx)
        X = ctx.enter_context(nc.sbuf_tensor("X", [P, s.NB, D], F32))
        ident = ctx.enter_context(nc.sbuf_tensor("ident", [P, P], F32))
        minus_half = ctx.enter_context(nc.sbuf_tensor("minus_half", [P, GB], F32))
        load_residual(nc, sems, s, a["x"], X, ident, minus_half)
        w_qkv, b_qkv = a["L0_xattn_w_qkv"], a["L0_xattn_b_qkv"]
        attention_phase(
            nc, sems, s, "self", X, ident, minus_half, cross=False, grouped=False, eps=1e-5, ctx_in=None,
            mask_in=a["mask_1x1xSxS2_fc1"], mask_multiplies=True, mask_per_sequence=False,
            weights=(w_qkv[:, 0:D], w_qkv[:, D:2 * D], w_qkv[:, 2 * D:3 * D], a["L0_xattn_w_ao"]),
            bias_q=b_qkv[0:D], bias_k=b_qkv[D:2 * D], bias_v=b_qkv[2 * D:3 * D], bias_o=a["L0_xattn_b_ao"],
            ln_s=a["L0_xattn_ln1_s"], ln_b=a["L0_xattn_ln1_b"], scale=32 ** -0.5, finish=None)
        sems.clear()
        w_kv, b_kv = a["L0_xattn_w_kv"], a["L0_xattn_b_kv"]
        attention_phase(
            nc, sems, s, "cross", X, ident, minus_half, cross=True, grouped=False, eps=1e-5, ctx_in=a["ctx_2048"],
            mask_in=a["mask_Bx1xSxS2_ff1"], mask_multiplies=True, mask_per_sequence=True,
            weights=(a["L0_xattn_w_q"], w_kv[:, 0:D], w_kv[:, D:2 * D], a["L0_xattn_w_co"]),
            bias_q=a["L0_xattn_b_q"], bias_k=b_kv[0:D], bias_v=b_kv[D:2 * D], bias_o=a["L0_xattn_b_co"],
            ln_s=a["L0_xattn_ln2_s"], ln_b=a["L0_xattn_ln2_b"], scale=32 ** -0.5, finish=None)
        sems.clear()
        mlp_phase(nc, sems, s, X, ident, minus_half, eps=1e-5, w1=a["L0_xattn_w1"], b1=a["L0_xattn_b1"],
                  w2=a["L0_xattn_w2"], b2=a["L0_xattn_b2"], ln_s=a["L0_xattn_ln3_s"], ln_b=a["L0_xattn_ln3_b"])
        sems.clear()
        attention_phase(
            nc, sems, s, "grouped", X, ident, minus_half, cross=True, grouped=True, eps=None, ctx_in=a["ctx_2048"],
            mask_in=a["mask_Bx1xSxS2_ff0"], mask_multiplies=False, mask_per_sequence=True,
            weights=(a["L1_xattn_Wq"], a["L1_xattn_Wk"], a["L1_xattn_Wv"], a["L1_xattn_Wo"]),
            bias_q=a["L1_xattn_bq"], bias_k=a["L1_xattn_bk"], bias_v=a["L1_xattn_bv"], bias_o=a["L1_xattn_bo"],
            ln_s=None, ln_b=None, scale=16 ** -0.5,
            finish=(a["L1_xattn_gamma"], a["L1_xattn_beta"], 1e-6, out))


def kernel(**inputs):
    import numpy as np
    import concourse.bacc as bacc
    from concourse.bass_utils import run_bass_kernel_spmd

    nc = bacc.Bacc("TRN2", target_bir_lowering=False, num_devices=1)
    arrays, args = {}, {}
    for name, value in inputs.items():
        a = np.ascontiguousarray(value)
        arrays[f"in_{name}_dram"] = a
        args[name] = nc.dram_tensor(f"in_{name}_dram", a.shape, mybir.dt.from_np(a.dtype), kind="ExternalInput").ap()
    x = arrays["in_x_dram"]
    out = nc.dram_tensor("out_dram", x.shape, mybir.dt.from_np(x.dtype), kind="ExternalOutput").ap()
    build_cross_attention_layers(nc, args, out)
    r = run_bass_kernel_spmd(nc, [arrays], core_ids=[0])
    return r.results[0]["out_dram"]
```

```python
from contextlib import ExitStack

import concourse.bass as bass
from concourse import mybir

F32 = mybir.dt.float32
F32R = mybir.dt.float32r
ALU = mybir.AluOpType
ACT = mybir.ActivationFunctionType
AX = mybir.AxisListType

P = 128
QUAD = 32
GB = 2
TOK = GB * P
BANK = 512
UH = 8
AHEAD = 24


def at(n):
    return n + (1 + AHEAD)


def over_groups(eng, count, body, first=0):
    with eng.Fori(first // 2, count // 2 - 1) as i:
        body(2 * i, 0, 2)
        body(2 * i + 1, 1, 2)
    body(count - 2, 0, 1)
    body(count - 1, 1, 0)


class Semaphores:

    def __init__(self, nc, ctx):
        self.nc, self.ctx, self.by_name = nc, ctx, {}

    def named(self, name):
        if name not in self.by_name:
            self.by_name[name] = self.ctx.enter_context(self.nc.semaphore(name))
        return self.by_name[name]

    def clear(self):
        with self.nc.Block() as block:
            @block.sync
            def _(sp):
                for done in self.by_name.values():
                    sp.sem_clear(done)


class Shape:

    def __init__(self, x, w1):
        self.NB, self.S, self.D = x.shape
        self.C = self.D // P
        self.G = self.NB // GB
        self.F = w1.shape[1]
        self.M = self.F // P


def column(v):
    return v.rearrange("(c p) -> p c", p=P)


def weight(w):
    return w.rearrange("(k p) n -> p k n", p=P)


class Weights:

    def __init__(self, nc, sems, stage, units):
        self.nc, self.stage, self.units, self.stages = nc, stage, units, stage.shape[1]
        self.loaded = [sems.named(f"weight_loaded{i}") for i in range(self.stages)]
        self.high_done, self.low_done = sems.named("weight_high"), sems.named("weight_low")

    def staged(self, i):
        k, n = self.units[i][0].shape[1:]
        return self.stage[:, i % self.stages, 0:k * n].rearrange("p (k n) -> p k n", k=k)

    def load(self, eng, i):
        if i >= self.stages:
            eng.wait_ge(self.low_done, i - self.stages + 1)
        eng.dma_start(self.staged(i), self.units[i][0]).then_inc(self.loaded[i % self.stages], 16)

    def round_high(self, act, i):
        act.wait_ge(self.loaded[i % self.stages], 16 * (i // self.stages + 1))
        self.nc.scalar.copy(self.units[i][1], self.staged(i)).then_inc(self.high_done, 1)

    def subtract_high(self, dve, i):
        src, high, low = self.units[i]
        dve.wait_ge(self.high_done, i + 1)
        self.nc.vector.tensor_tensor(low, self.staged(i), high.bitcast(F32), ALU.subtract).then_inc(self.low_done, 1)

    def wait_split(self, pe, i):
        pe.wait_ge(self.low_done, i + 1)


def project(nc, out, stationary, moving, chunks):
    for c in range(chunks):
        for n, (a, b) in enumerate(((1, 0), (0, 1), (0, 0))):
            mm = nc.tensor.matmul(out, stationary(c, a), moving(c, b),
                                  start=c == 0 and n == 0, stop=c == chunks - 1 and n == 2)
    return mm


def attention_phase(nc, sems, s, name, X, ident, minus_half, *, x_in=None, cross, grouped, eps, ctx_in, mask_in, mask_multiplies,
                    mask_per_sequence, weights, bias_q, bias_k, bias_v, bias_o, ln_s, ln_b,
                    scale, finish):
    wq, wk, wv, wo = weights
    D, C, G = s.D, s.C, s.G
    kd = wk.shape[1]
    KJ = kd // P
    HD = 16 if grouped else 32
    KVH = kd // HD
    U = GB * (D // HD) // UH
    UB = U // GB
    SHARE = D // kd
    LEAD = 3 if grouped else 2
    HALF = SHARE * HD
    VPAD = HALF - HD if grouped else 0
    VW = HD + 2 * VPAD

    if grouped:
        jobs = [("k", 0)] + [("q", m) for m in range(C)] + [("v", b) for b in range(GB)]
        before = {0: jobs[0:1], 1: jobs[1:2], 2: jobs[2:3], 3: jobs[3:4], 4: jobs[4:5], 5: jobs[5:6], 6: jobs[6:7]}
        after = {}
    else:
        jobs = [("k", m) for m in range(KJ)] + [("q", m) for m in range(C)] + [("v", b) for b in range(GB)]
        before = {0: jobs[0:2], 1: jobs[4:6], 2: jobs[8:9], U - 1: jobs[9:10]}
        after = {0: jobs[2:4], 1: jobs[6:8]}
    job_bank = {job: 6 + j % 2 for j, job in enumerate(jobs)}
    job_before = {job: jobs[j - 2] if j >= 2 else None for j, job in enumerate(jobs)}

    with ExitStack() as ctx:
        def sb(n, shape, dt=F32):
            return ctx.enter_context(nc.sbuf_tensor(f"{name}_{n}", shape, dt))

        def sem(n):
            return sems.named(n)

        Wq = [sb(f"Wq{h}", [P, C, D], F32R) for h in "hl"]
        Wk = [sb(f"Wk{h}", [P, C, kd], F32R) for h in "hl"]
        Wv = [sb(f"Wv{h}", [P, C, kd], F32R) for h in "hl"]
        Wo = [sb(f"Wo{h}", [P, C, D], F32R) for h in "hl"]
        weights = Weights(nc, sems, sb("stage", [P, 2, C * D]), [
                                     (weight(wk), Wk[0][:, :, :], Wk[1][:, :, :]),
                                     (weight(wq), Wq[0][:, :, :], Wq[1][:, :, :]),
                                     (weight(wv), Wv[0][:, :, :], Wv[1][:, :, :]),
                                     (weight(wo), Wo[0][:, :, :], Wo[1][:, :, :])])
        FOR_K, FOR_Q, FOR_V, FOR_O = range(4)
        row_bias = sb("row_bias", [P, D])
        v_bias = sb("v_bias", [P, kd])

        xT = [sb(f"xT{h}", [P, C, TOK], F32R) for h in "hl"]
        cT = [sb(f"cT{h}", [P, C, TOK], F32R) for h in "hl"] if cross else xT
        zs = sb("zs", [P, GB, D])
        if not grouped:
            affine = sb("affine", [P, GB, C, P])
            ln_cols = sb("ln_cols", [P, 2, C])
        stats = sb("stats", [P, GB, 6])
        tick = sb("tick", [P, 2])
        mean_var = sb("mean_var", [P, GB, 4])
        ctx_rows = sb("ctx_rows", [P, GB, D]) if cross else None
        qT = sb("qT", [P, 2, C, TOK])
        if grouped:
            k_raw = sb("k_raw", [P, TOK])
            kT = sb("kT", [P, 2, C, GB, SHARE, P])
        else:
            kT = sb("kT", [P, 2, C, TOK])
        V = sb("V", [P, 2, GB, KVH, VW])
        t = sb("t", [P, 4, 2, 4, P])
        pT = sb("pT", [P, 2, 4, P])
        neg_max = sb("neg_max", [P, 4, UH])
        sums = sb("sums", [P, 4, UH])
        recip = sb("recip", [P, 4, UH])
        minus_one = sb("minus_one", [P, UH])
        oT = [sb(f"oT{h}", [P, C, P], F32R) for h in "hl"]
        NM = 2 * GB if mask_per_sequence else 1
        mask = sb("mask", [P, NM, P])
        mask_add = sb("mask_add", [P, NM, P]) if mask_multiplies else None
        bq = sb("bq", [P, C])
        bk = sb("bk", [P, KJ])
        if finish:
            y = sb("y", [P, GB, D])
            fstats = sb("fstats", [P, GB, 6])
            fmv = sb("fmv", [P, GB, 4])
            gamma = sb("gamma", [P, D])
            beta = sb("beta", [P, D])

        score_ps = ctx.enter_context(nc.psum_tensor(f"{name}_scores", [P, 2, BANK], F32))
        other_ps = ctx.enter_context(nc.psum_tensor(f"{name}_others", [P, 6, BANK], F32))

        def bank(i):
            return other_ps[:, i - 2, :]

        def chunks(ap):
            return ap.rearrange("p (c k) -> p c k", k=P)

        small_in = sem("small_in")
        SMALL = 16 * (5 if finish else 3)
        bk_in = sem("bk_in")
        ln_in = sem("ln_in")
        x_loaded = [sem(f"x_loaded{i}") for i in range(3)]
        mask_loaded = [sem(f"mask_loaded{i}") for i in range(2)]
        ctx_loaded = sem("ctx_loaded")
        values_cleared = sem("values_cleared")
        rows_cleared = sem("rows_cleared")
        stats_done, aggr_done, eps_added, rstd_done, z_done = (
            sem(n) for n in ("stats_done", "aggr_done", "eps_added", "rstd_done", "z_done"))
        mask_ready = sem("mask_ready")
        row_added = sem("row_added")
        ctx_turned, x_turned = sem("ctx_turned"), sem("x_turned")
        c_high, c_low = sem("c_high"), sem("c_low")
        x_affine, x_high, x_low = sem("x_affine"), sem("x_high"), sem("x_low")
        made = {"k": sem("k_made"), "q": sem("q_made"), "v": sem("v_made")}
        kept = {"k": sem("k_kept"), "q": sem("q_kept"), "v": sem("v_kept")}
        per = {"k": KJ, "q": C, "v": GB}
        k_placed = sem("k_placed")
        if grouped:
            k_stored = sem("k_stored")
            k_dram = nc.dram_tensor("keys", (2 * HD, C, TOK), F32).ap()
        scores_made, scores_read, mask_added, max_done, exp_done, probs_done = (
            sem(n) for n in ("scores_made", "scores_read", "mask_added", "max_done", "exp_done", "probs_done"))
        probs_turned, pT_a, pT_b = sem("probs_turned"), sem("pT_a"), sem("pT_b")
        exponent_set = sem("exponent_set")
        recip_done, out_made = sem("recip_done"), sem("out_made")
        o_high, o_low = sem("o_high"), sem("o_low")
        final_made, x_added = sem("final_made"), sem("x_added")
        if finish:
            f_stats, f_aggr, f_eps, f_rstd, f_z, f_scaled, f_shifted = (
                sem(n) for n in ("f_stats", "f_aggr", "f_eps", "f_rstd", "f_z", "f_scaled", "f_shifted"))
            stored = [sem(f"stored{i}") for i in range(GB)]

        PLACED = 16 * 2 * SHARE
        block = ctx.enter_context(nc.Block())

        def value_head(r, i):
            return 2 * (2 * (r // 2) + i // 4) + r % 2 if grouped else 4 * (i % 4) + 2 * r + i // 4

        def ahead(g, par, u):
            return (g, par, u + LEAD) if u + LEAD < U else (g + 1, 1 - par, u + LEAD - U)

        @block.sync
        def _(sp):
            def load_context(g):
                sp.wait_ge(ctx_turned, at(g * GB - 1))
                sp.dma_start(ctx_rows[:, :, :],
                             ctx_in[bass.ds(g * GB, GB), :, :].rearrange("b p d -> p b d")).then_inc(ctx_loaded, 16)

            def load_x(g):
                sp.dma_start(X[:, g * GB:(g + 1) * GB, :],
                             x_in[g * GB:(g + 1) * GB, :, :].rearrange("b p d -> p b d")
                             ).then_inc(x_loaded[min(g, 2)], 16)

            if finish:
                for done in stored:
                    sp.sem_inc(done, 16)
            sp.sem_inc(k_placed, 16)
            if cross:
                load_context(0)
            if x_in is not None:
                load_x(0)
            sp.dma_start(bk[:, :], column(bias_k), allow_slow_non_contiguous=True).then_inc(bk_in, 16)
            if not grouped:
                sp.dma_start(ln_cols[:, 0, :], column(ln_s), allow_slow_non_contiguous=True).then_inc(ln_in, 16)
                sp.dma_start(ln_cols[:, 1, :], column(ln_b), allow_slow_non_contiguous=True).then_inc(ln_in, 16)
            weights.load(sp, FOR_K)
            sp.dma_start(bq[:, :], column(bias_q), allow_slow_non_contiguous=True).then_inc(small_in, 16)
            if finish:
                sp.dma_start(gamma[:, :], finish[0].partition_broadcast(P)).then_inc(small_in, 16)
                sp.dma_start(beta[:, :], finish[1].partition_broadcast(P)).then_inc(small_in, 16)
            sp.dma_start(row_bias[:, :], bias_o.partition_broadcast(P)).then_inc(small_in, 16)
            sp.dma_start(v_bias[:, :], bias_v.partition_broadcast(P)).then_inc(small_in, 16)
            if not mask_per_sequence:
                sp.dma_start(mask[:, 0, :], mask_in[0, 0, :, :]).then_inc(mask_loaded[0], 16)

            def load_mask(g, par):
                sp.wait_ge(scores_read, at((g - 1) * U - 1))
                sp.dma_start(mask[:, par * GB:(par + 1) * GB, :], mask_in[bass.ds(g * GB, GB), 0, :, :].rearrange(
                    "b p k -> p b k")).then_inc(mask_loaded[par], 16)

            def place_keys(g, par):
                sp.wait_ge(kept["k"], at(g))
                sp.wait_ge(scores_made, at((g - 1) * U - 1))
                sp.wait_ge(rows_cleared, 1)
                sp.wait_ge(k_placed, PLACED * g + 16)
                sp.dma_start(k_dram.rearrange("n c t -> c n t"), k_raw[:, :]).then_inc(k_stored, 16)
                sp.wait_ge(k_stored, 16 * g + 16)
                for half in range(2):
                    for e in range(SHARE):
                        row = HALF * half + HD * e
                        sp.dma_start(
                            kT[row:row + HD, par, :, :, e, :].rearrange("p c b k -> p (c b) k"),
                            k_dram[half * HD:(half + 1) * HD, :, :].rearrange("r c (b k) -> r (c b) k", b=GB)
                        ).then_inc(k_placed, 16)

            weights.load(sp, FOR_Q)
            if x_in is not None:
                load_x(1)
            def store(g, b):
                sp.wait_ge(f_shifted, at(g * GB + b))
                sp.dma_start(finish[3][bass.ds(g * GB + b, 1), :, :].rearrange("b p d -> p b d"),
                             y[:, b:b + 1, :]).then_inc(stored[b], 16)

            if mask_per_sequence:
                load_mask(0, 0)
            weights.load(sp, FOR_V)
            if cross:
                load_context(1)
            weights.load(sp, FOR_O)
            if x_in is not None:
                for g in range(2, G):
                    load_x(g)
            if grouped:
                place_keys(0, 0)

            def body(g, par, left, first=False):
                if mask_per_sequence and left >= 1:
                    load_mask(g + 1, 1 - par)
                if cross and left >= 2:
                    load_context(g + 2)
                if grouped and left >= 1:
                    place_keys(g + 1, 1 - par)
                if finish:
                    if not first:
                        store(g - 1, 1)
                    store(g, 0)
                    if not left:
                        store(g, 1)

            if cross:
                body(0, 0, 2, first=True)
                body(1, 1, 2)
                over_groups(sp, G, body, first=2)
            if finish:
                for b in range(GB):
                    sp.wait_ge(stored[b], 16 * (G + 1))

        @block.gpsimd
        def _(pool):
            for done in (rstd_done, row_added, mask_added, recip_done, probs_done):
                pool.sem_inc(done, AHEAD)
            if finish:
                for done in (f_rstd, f_scaled, f_shifted):
                    pool.sem_inc(done, AHEAD)
            nc.gpsimd.memset(minus_one[:, :], -1.0).then_inc(exponent_set, 1)
            pool.wait_ge(exponent_set, 1)
            if grouped:
                nc.gpsimd.memset(kT[:, :, :, :, :, :].rearrange("p a c b e k -> p (a c b e k)"),
                                 0.0).then_inc(rows_cleared, 1)

            def root(g):
                pool.wait_ge(eps_added, at(g))
                nc.gpsimd.tensor_tensor(mean_var[:, :, 3], mean_var[:, :, 2], minus_half[:, 0:GB],
                                        ALU.pow).then_inc(rstd_done, 1)

            def add_row_bias(g, b):
                pool.wait_ge(z_done, at(g * GB + b))
                xb = X[:, bass.ds(g * GB + b, 1), :].rearrange("p b d -> p (b d)")
                nc.gpsimd.tensor_tensor(xb, xb, row_bias[:, :], ALU.add).then_inc(row_added, 1)

            def add_mask(g, par, u):
                n = g * U + u
                pool.wait_ge(scores_read, at(n))
                if u == 0:
                    pool.wait_ge(mask_ready, at(g if mask_per_sequence else 0))
                m = par * GB + u // UB if mask_per_sequence else 0
                tu = t[:, u % 4, :, :, :].rearrange("p a c k -> p (a c) k")
                nc.gpsimd.tensor_tensor(tu, tu, mask_add[:, m:m + 1, :].to_broadcast([P, UH, P]),
                                        ALU.add).then_inc(mask_added, 1)

            def divide(n, u):
                pool.wait_ge(exp_done, at(2 * n + 1))
                nc.gpsimd.tensor_tensor(recip[:, u % 4, :], sums[:, u % 4, :], minus_one[:, :],
                                        ALU.pow).then_inc(recip_done, 1)
                pool.wait_ge(recip_done, at(n))
                for sl in range(2):
                    tu = t[:, u % 4, sl, :, :]
                    nc.gpsimd.tensor_tensor(tu, tu, recip[:, u % 4, 4 * sl:4 * sl + 4].unsqueeze(2).to_broadcast(
                        [P, 4, P]), ALU.mult).then_inc(probs_done, 1)

            def finish_row(g, b):
                pool.wait_ge(f_eps, at(g * GB + b))
                nc.gpsimd.tensor_tensor(fmv[:, b, 3:4], fmv[:, b, 2:3], minus_half[:, 0:1],
                                        ALU.pow).then_inc(f_rstd, 1)
                pool.wait_ge(f_z, at(g * GB + b))
                yb = y[:, b, :]
                nc.gpsimd.tensor_tensor(yb, yb, gamma[:, :], ALU.mult).then_inc(f_scaled, 1)
                pool.wait_ge(f_scaled, at(g * GB + b))
                nc.gpsimd.tensor_tensor(yb, yb, beta[:, :], ALU.add).then_inc(f_shifted, 1)

            if not grouped:
                root(0)
                root(1)
            pool.wait_ge(small_in, SMALL)
            for b in range(GB):
                add_row_bias(0, b)
            if mask_multiplies:
                for u in range(LEAD):
                    add_mask(0, 0, u)
            divide(0, 0)

            def body(g, par, left, first=False):
                for u in range(U):
                    if mask_multiplies and (left or u + LEAD < U):
                        add_mask(*ahead(g, par, u))
                    if left or u + 1 < U:
                        divide(g * U + u + 1, u + 1)
                    if u < GB and left:
                        add_row_bias(g + 1, u)
                    if finish and u == 1 and not first:
                        finish_row(g - 1, 1)
                    if finish and u == UB + 1:
                        finish_row(g, 0)
                    if u == 0 and not grouped and left >= 2:
                        root(g + 2)
                if finish and not left:
                    finish_row(g, 1)

            body(0, 0, 2, first=True)
            body(1, 1, 2)
            over_groups(pool, G, body, first=2)

        @block.scalar
        def _(act):
            for done in (c_high, x_affine, kept["k"], exp_done, pT_a, o_high):
                act.sem_inc(done, AHEAD)
            if grouped:
                act.sem_inc(x_high, AHEAD)

            def context_high(g):
                for b in range(GB):
                    act.wait_ge(ctx_turned, at(g * GB + b))
                    if b == 0:
                        act.wait_ge(made["v"], at(g * GB - 1))
                    nc.scalar.copy(cT[0][:, :, b * P:(b + 1) * P], chunks(bank(6 + b))).then_inc(c_high, 1)

            def rows_high(g):
                for b in range(GB):
                    act.wait_ge(x_turned, at(g * GB + b))
                    if grouped:
                        if b == 0:
                            act.wait_ge(made["q"], at(g * C - 1))
                        nc.scalar.copy(xT[0][:, :, b * P:(b + 1) * P], chunks(bank(6 + b))).then_inc(x_high, 1)
                    else:
                        act.wait_ge(x_low, at((g - 1) * GB + b))
                        for c in range(C):
                            ins = nc.scalar.activation(
                                affine[:, b, c, :], bank(6 + b)[:, c * P:(c + 1) * P], ACT.Identity,
                                bias=ln_cols[:, 1, c:c + 1], scale=ln_cols[:, 0, c:c + 1])
                        ins.then_inc(x_affine, 1)

            def keep_keys(g, par, job):
                kind, m = job
                if kind != "k":
                    return
                act.wait_ge(made[kind], at(g * per[kind] + m))
                src = bank(job_bank[job])
                if m == 0:
                    act.wait_ge(scores_made, at((g - 1) * U - 1))
                    if grouped:
                        act.wait_ge(k_placed, PLACED * g + 16)
                dst = k_raw[:, :] if grouped else kT[:, par, m, :]
                nc.scalar.activation(dst, src[:, 0:TOK], ACT.Identity, bias=bk[:, m:m + 1]).then_inc(kept["k"], 1)

            def probabilities(g, par, u):
                act.wait_ge(max_done, at(g * U + u))
                tu = t[:, u % 4, :, :, :].rearrange("p a c k -> p (a c) k")
                for i in range(UH):
                    ins = nc.scalar.activation(tu[:, i, :], tu[:, i, :], ACT.Exp, bias=neg_max[:, u % 4, i:i + 1],
                                               accum_out=sums[:, u % 4, i:i + 1])
                    if i % 4 == 3:
                        ins.then_inc(exp_done, 1)

            def output_high(g, b):
                n = g * GB + b
                act.wait_ge(out_made, at(g * U + (b + 1) * UB - 1))
                act.wait_ge(final_made, at(n - 1))
                nc.scalar.copy(oT[0][:, :, :], chunks(bank(4))).then_inc(o_high, 1)

            if cross:
                context_high(0)
            else:
                act.wait_ge(ln_in, 16 * 2)
                rows_high(0)
            weights.round_high(act, FOR_K)
            act.wait_ge(bk_in, 16)
            for job in jobs[0:2]:
                keep_keys(0, 0, job)
            weights.round_high(act, FOR_Q)
            for job in jobs[2:4]:
                keep_keys(0, 0, job)
            if cross:
                if not grouped:
                    act.wait_ge(ln_in, 16 * 2)
                rows_high(0)
            weights.round_high(act, FOR_V)
            weights.round_high(act, FOR_O)
            if cross:
                context_high(1)
            else:
                rows_high(1)
            for u in range(LEAD):
                probabilities(0, 0, u)

            def body(g, par, left, first=False):
                for u in range(U):
                    n = g * U + u
                    act.wait_ge(probs_turned, at(2 * n))
                    act.wait_ge(out_made, at(n - 1))
                    nc.scalar.copy(pT[:, 0, :, :], chunks(bank(2))).then_inc(pT_a, 1)
                    if cross and left and u == 0:
                        rows_high(g + 1)
                    if left:
                        for job in before.get(u, ()):
                            keep_keys(g + 1, 1 - par, job)
                    if u == UB - 1:
                        output_high(g, 0)
                    if u == U - 1:
                        output_high(g, 1)
                        if cross and left >= 2:
                            context_high(g + 2)
                        elif left >= 2:
                            rows_high(g + 2)
                    if left or u + LEAD < U:
                        probabilities(*ahead(g, par, u))
                    if left:
                        for job in after.get(u, ()):
                            keep_keys(g + 1, 1 - par, job)

            body(0, 0, 2, first=True)
            body(1, 1, 2)
            over_groups(act, G, body, first=2)

        @block.vector
        def _(dve):
            for done in (c_low, x_low, kept["q"], kept["v"], scores_read, max_done, pT_b, o_low, x_added, z_done,
                         stats_done, aggr_done, eps_added, mask_ready):
                dve.sem_inc(done, AHEAD)
            if not grouped:
                dve.sem_inc(x_high, AHEAD)
            if finish:
                for done in (f_stats, f_aggr, f_eps, f_z):
                    dve.sem_inc(done, AHEAD)
            if grouped:
                nc.vector.memset(V[:, :, :, :, :].rearrange("p a b h o -> p (a b h o)"), 0.0).then_inc(
                    values_cleared, 1)
                dve.wait_ge(values_cleared, 1)

            def x_row(g, b):
                return X[:, bass.ds(g * GB + b, 1), :].rearrange("p b d -> p (b d)")

            def statistics(g):
                if grouped:
                    return
                if x_in is not None:
                    if isinstance(g, int) and g < 2:
                        dve.wait_ge(x_loaded[g], 16)
                    else:
                        dve.wait_ge(x_loaded[2], 16 * (G - 2))
                for b in range(GB):
                    nc.vector.bn_stats(stats[:, b, :], x_row(g, b)).then_inc(stats_done, 1)
                dve.wait_ge(stats_done, at(g * GB + GB - 1))
                nc.vector.memset(tick[:, 0:1], 0.0)
                for b in range(GB):
                    nc.vector.bn_aggr(mean_var[:, b, 0:2], stats[:, b, :]).then_inc(aggr_done, 1)
                dve.wait_ge(aggr_done, at(g * GB + GB - 1))
                nc.vector.tensor_scalar(mean_var[:, :, 2], mean_var[:, :, 1], eps, None,
                                        ALU.add).then_inc(eps_added, 1)

            def normalise(g):
                dve.wait_ge(x_turned, at(g * GB - 1))
                if grouped:
                    for b in range(GB):
                        nc.vector.tensor_copy(zs[:, b, :], x_row(g, b)).then_inc(z_done, 1)
                    return
                dve.wait_ge(rstd_done, at(g))
                for b in range(GB):
                    nc.vector.tensor_scalar(zs[:, b, :], x_row(g, b), mean_var[:, b, 0:1], mean_var[:, b, 3:4],
                                            ALU.subtract, ALU.mult).then_inc(z_done, 1)

            def context_low(g):
                if not cross:
                    return
                for b in range(GB):
                    dve.wait_ge(c_high, at(g * GB + b))
                    tok = slice(b * P, (b + 1) * P)
                    nc.vector.tensor_tensor(cT[1][:, :, tok], chunks(bank(6 + b)),
                                            cT[0][:, :, tok].bitcast(F32), ALU.subtract).then_inc(c_low, 1)

            def x_halves(g):
                for b in range(GB):
                    tok = slice(b * P, (b + 1) * P)
                    if grouped:
                        dve.wait_ge(x_high, at(g * GB + b))
                        nc.vector.tensor_tensor(xT[1][:, :, tok], chunks(bank(6 + b)),
                                                xT[0][:, :, tok].bitcast(F32), ALU.subtract).then_inc(x_low, 1)
                        continue
                    dve.wait_ge(x_affine, at(g * GB + b))
                    if b == 0:
                        dve.wait_ge(made["q"], at(g * C - 1))
                        if not cross:
                            dve.wait_ge(made["v"], at(g * GB - 1))
                    nc.vector.tensor_copy(xT[0][:, :, tok], affine[:, b, :, :]).then_inc(x_high, 1)
                    dve.wait_ge(x_high, at(g * GB + b))
                    nc.vector.tensor_tensor(xT[1][:, :, tok], affine[:, b, :, :],
                                            xT[0][:, :, tok].bitcast(F32), ALU.subtract).then_inc(x_low, 1)

            def keep(g, par, job):
                kind, m = job
                if kind == "k":
                    return
                dve.wait_ge(made[kind], at(g * per[kind] + m))
                src = bank(job_bank[job])
                if kind == "q":
                    if m == 0:
                        dve.wait_ge(scores_made, at((g - 1) * U - 1))
                    nc.vector.tensor_scalar(qT[:, par, m, :], src[:, 0:TOK], bq[:, m:m + 1], scale,
                                            ALU.add, ALU.mult).then_inc(kept["q"], 1)
                else:
                    if m == 0:
                        dve.wait_ge(out_made, at((g - 1) * U - 1))
                    nc.vector.tensor_tensor(V[:, par, m, :, VPAD:VPAD + HD], src[:, 0:kd].rearrange("p (h d) -> p h d", h=KVH),
                                            v_bias[:, :].rearrange("p (h d) -> p h d", h=KVH),
                                            ALU.add).then_inc(kept["v"], 1)

            def prepare_mask(g, par):
                if mask_multiplies and mask_per_sequence:
                    dve.wait_ge(mask_loaded[par], 8 * (g - par) + 16)
                    dve.wait_ge(mask_added, at((g - 1) * U - 1))
                    m = slice(par * GB, (par + 1) * GB)
                    nc.vector.tensor_scalar(mask_add[:, m, :], mask[:, m, :], 1.0, 10000.0,
                                            ALU.subtract, ALU.mult).then_inc(mask_ready, 1)

            def read_scores(g, par, u):
                n = g * U + u
                dve.wait_ge(scores_made, at(n))
                dve.wait_ge(probs_turned, at(2 * (n - 4) + 1))
                m = 0
                if mask_per_sequence:
                    m = par * GB + u // UB
                    if u == 0:
                        dve.wait_ge(mask_loaded[par], 8 * (g - par) + 16)
                sc = score_ps[:, :, :].rearrange("p a (c k) -> p (a c) k", k=P)
                tu = t[:, u % 4, :, :, :].rearrange("p a c k -> p (a c) k")
                nc.vector.tensor_tensor(tu, sc, mask[:, m:m + 1, :].to_broadcast([P, UH, P]),
                                        ALU.mult if mask_multiplies else ALU.add).then_inc(scores_read, 1)

            def row_max(g, par, u):
                n = g * U + u
                dve.wait_ge(mask_added if mask_multiplies else scores_read, at(n))
                tu = t[:, u % 4, :, :, :].rearrange("p a c k -> p (a c) k")
                nc.vector.tensor_reduce(neg_max[:, u % 4, :], tu, AX.X, ALU.max, negate=True).then_inc(max_done, 1)

            def output_low(n):
                dve.wait_ge(o_high, at(n))
                nc.vector.tensor_tensor(oT[1][:, :, :], chunks(bank(4)), oT[0][:, :, :].bitcast(F32),
                                        ALU.subtract).then_inc(o_low, 1)

            def add_output(g, b):
                n = g * GB + b
                dve.wait_ge(final_made, at(n))
                dve.wait_ge(row_added, at(n))
                if not finish:
                    nc.vector.tensor_tensor(x_row(g, b), bank(5), x_row(g, b), ALU.add).then_inc(x_added, 1)
                    return
                yb = y[:, b, :]
                dve.wait_ge(stored[b], 16 * g + 16)
                nc.vector.tensor_tensor(yb, bank(5), x_row(g, b), ALU.add).then_inc(x_added, 1)
                dve.wait_ge(x_added, at(n))
                nc.vector.bn_stats(fstats[:, b, :], yb).then_inc(f_stats, 1)
                dve.wait_ge(f_stats, at(n))
                nc.vector.memset(tick[:, b:b + 1], 0.0)
                nc.vector.bn_aggr(fmv[:, b, 0:2], fstats[:, b, :]).then_inc(f_aggr, 1)
                dve.wait_ge(f_aggr, at(n))
                nc.vector.tensor_scalar(fmv[:, b, 2:3], fmv[:, b, 1:2], finish[2], None, ALU.add).then_inc(f_eps, 1)

            def finish_row(g, b):
                if finish:
                    dve.wait_ge(f_rstd, at(g * GB + b))
                    yb = y[:, b, :]
                    nc.vector.tensor_scalar(yb, yb, fmv[:, b, 0:1], fmv[:, b, 3:4], ALU.subtract,
                                            ALU.mult).then_inc(f_z, 1)

            statistics(0)
            context_low(0)
            normalise(0)
            if cross:
                weights.subtract_high(dve, FOR_K)
                statistics(1)
                weights.subtract_high(dve, FOR_Q)
                x_halves(0)
            else:
                x_halves(0)
                weights.subtract_high(dve, FOR_K)
                weights.subtract_high(dve, FOR_Q)
                statistics(1)
            dve.wait_ge(small_in, SMALL)
            if mask_multiplies and not mask_per_sequence:
                dve.wait_ge(mask_loaded[0], 16)
                nc.vector.tensor_scalar(mask_add[:, :, :], mask[:, :, :], 1.0, 10000.0,
                                        ALU.subtract, ALU.mult).then_inc(mask_ready, 1)
            prepare_mask(0, 0)
            for n, job in enumerate(jobs):
                if n == KJ + 2:
                    weights.subtract_high(dve, FOR_V)
                if job[0] == "v" and job[1] == 0:
                    normalise(1)
                keep(0, 0, job)
            weights.subtract_high(dve, FOR_O)
            read_scores(0, 0, 0)
            if not mask_multiplies:
                row_max(0, 0, 0)
            context_low(1)
            if not cross:
                x_halves(1)
            for u in range(1, LEAD):
                read_scores(0, 0, u)
                if not mask_multiplies:
                    row_max(0, 0, u)
            if mask_multiplies:
                for u in range(LEAD):
                    row_max(0, 0, u)

            def body(g, par, left, first=False):
                for u in range(U):
                    n = g * U + u
                    more = left or u + LEAD < U
                    if u == UB:
                        output_low(g * GB)
                    if more:
                        read_scores(*ahead(g, par, u))
                    dve.wait_ge(probs_turned, at(2 * n + 1))
                    dve.wait_ge(out_made, at(n - 1))
                    nc.vector.tensor_copy(pT[:, 1, :, :], chunks(bank(3))).then_inc(pT_b, 1)
                    if more and not mask_multiplies:
                        row_max(*ahead(g, par, u))
                    if u == 0 and left:
                        prepare_mask(g + 1, 1 - par)
                        if cross:
                            x_halves(g + 1)
                    if left:
                        for job in before.get(u, ()):
                            keep(g + 1, 1 - par, job)
                    if not cross and u == U - 1:
                        output_low(g * GB + 1)
                    if more and mask_multiplies:
                        row_max(*ahead(g, par, u))
                    if u == 0 and not first:
                        add_output(g - 1, 1)
                    if u == 1 and not first:
                        finish_row(g - 1, 1)
                    if u == UB:
                        add_output(g, 0)
                    if u == min(UB + 1, U - 1):
                        finish_row(g, 0)
                    if left:
                        for job in after.get(u, ()):
                            keep(g + 1, 1 - par, job)
                    if u == 0 and left >= 2:
                        statistics(g + 2)
                    if u == U - 2 and left >= 2:
                        normalise(g + 2)
                if cross:
                    output_low(g * GB + 1)
                if left >= 2:
                    context_low(g + 2)
                    if not cross:
                        x_halves(g + 2)
                if not left:
                    add_output(g, 1)
                    finish_row(g, 1)

            body(0, 0, 2, first=True)
            body(1, 1, 2)
            over_groups(dve, G, body, first=2)

        @block.tensor
        def _(pe):
            for done in (ctx_turned, x_turned, made["k"], made["q"], made["v"], scores_made, probs_turned, out_made,
                         final_made):
                pe.sem_inc(done, AHEAD)

            def turn_context(g):
                if cross:
                    pe.wait_ge(kept["v"], at(g * GB - 1))
                    pe.wait_ge(ctx_loaded, 16 * g + 16)
                    for b in range(GB):
                        for c in range(C):
                            mm = nc.tensor.transpose(bank(6 + b)[:, c * P:(c + 1) * P],
                                                     ctx_rows[:, b, c * P:(c + 1) * P], ident[:, :])
                        mm.then_inc(ctx_turned, 1)

            def turn_rows(g):
                pe.wait_ge(kept["v"], at(g * GB - 1))
                for b in range(GB):
                    pe.wait_ge(z_done, at(g * GB + b))
                    if cross:
                        pe.wait_ge(c_low, at(g * GB + b))
                    for c in range(C):
                        mm = nc.tensor.transpose(bank(6 + b)[:, c * P:(c + 1) * P], zs[:, b, c * P:(c + 1) * P],
                                                 ident[:, :])
                    mm.then_inc(x_turned, 1)

            def make(g, par, job, before_rows=False):
                kind, m = job
                out = bank(job_bank[job])
                prev = job_before[job]
                if prev:
                    pe.wait_ge(kept[prev[0]], at(g * per[prev[0]] + prev[1]))
                elif not grouped and not before_rows:
                    pe.wait_ge(x_affine, at(g * GB + job_bank[job] - 6))
                if kind == "k" and m == 0 and cross:
                    pe.wait_ge(c_low, at(g * GB + GB - 1))
                    if grouped and not before_rows:
                        pe.wait_ge(x_low, at(g * GB + GB - 1))
                elif m == 0:
                    pe.wait_ge(x_low, at(g * GB + GB - 1))
                if m == 0:
                    weights.wait_split(pe, {"k": FOR_K, "q": FOR_Q, "v": FOR_V}[kind])
                if kind == "k":
                    mm = project(nc, out[:, 0:TOK], lambda c, h: Wk[h][:, c, m * P:(m + 1) * P],
                                 lambda c, h: cT[h][:, c, :], C)
                elif kind == "q":
                    mm = project(nc, out[:, 0:TOK], lambda c, h: Wq[h][:, c, m * P:(m + 1) * P],
                                 lambda c, h: xT[h][:, c, :], C)
                else:
                    mm = project(nc, out[:, 0:kd], lambda c, h: cT[h][:, c, m * P:(m + 1) * P],
                                 lambda c, h: Wv[h][:, c, :], C)
                mm.then_inc(made[kind], 1)

            def scores(g, par, u):
                b, r = u // UB, u % UB
                pe.wait_ge(scores_read, at(g * U + u - 1))
                if u == 0:
                    pe.wait_ge(kept["q"], at(g * C + C - 1))
                    if grouped:
                        pe.wait_ge(k_placed, PLACED * g + PLACED + 16)
                    else:
                        pe.wait_ge(kept["k"], at(g * KJ + KJ - 1))
                tok = slice(b * P, (b + 1) * P)
                if not grouped:
                    for i in (0, 4, 1, 5, 2, 6, 3, 7):
                        q, c = 2 * r + i // 4, i % 4
                        rows = slice(QUAD * q, QUAD * q + QUAD)
                        mm = nc.tensor.matmul(score_ps[:, i // 4, c * P:(c + 1) * P], qT[rows, par, c, tok],
                                              kT[rows, par, c, tok], start=True, stop=True)
                else:
                    for i in range(2):
                        c, rows = 2 * (r // 2) + i, slice(HALF * (r % 2), HALF * (r % 2) + HALF)
                        mm = nc.tensor.matmul(score_ps[:, i, :], qT[rows, par, c, tok],
                                              kT[rows, par, c, b, :, :].rearrange("p e k -> p (e k)"),
                                              start=True, stop=True)
                mm.then_inc(scores_made, 1)

            def turn_probs(n, u):
                for sl in range(2):
                    pe.wait_ge(probs_done, at(2 * n + sl))
                    pe.wait_ge(pT_b if sl else pT_a, at(n - 1))
                    for c in range(4):
                        mm = nc.tensor.transpose(bank(2 + sl)[:, c * P:(c + 1) * P], t[:, u % 4, sl, c, :],
                                                 ident[:, :])
                    mm.then_inc(probs_turned, 1)

            def outputs(g, par, u):
                n = g * U + u
                b, r = u // UB, u % UB
                pe.wait_ge(pT_a, at(n))
                if u == 0:
                    pe.wait_ge(kept["v"], at(g * GB + GB - 1))
                if r == 0:
                    pe.wait_ge(o_low, at(g * GB + b - 1))
                for i in range(UH):
                    if i == 4:
                        pe.wait_ge(pT_b, at(n))
                    v = V[:, par, b, value_head(r, i), :]
                    if grouped:
                        c, row, e = 2 * (r // 2) + i // 4, HALF * (r % 2), i % 4
                        mm = nc.tensor.matmul(bank(4)[row:row + HALF, c * P:(c + 1) * P],
                                              v[:, VPAD - HD * e:VPAD - HD * e + HALF], pT[:, i // 4, i % 4, :],
                                              start=e == 0, stop=e == SHARE - 1)
                    else:
                        c, row = i % 4, QUAD * (2 * r + i // 4)
                        mm = nc.tensor.matmul(bank(4)[row:row + QUAD, c * P:(c + 1) * P], v, pT[:, i // 4, i % 4, :],
                                              start=True, stop=True)
                mm.then_inc(out_made, 1)

            def project_output(n):
                pe.wait_ge(o_low, at(n))
                pe.wait_ge(x_added, at(n - 1))
                weights.wait_split(pe, FOR_O)
                project(nc, bank(5), lambda c, h: oT[h][:, c, :], lambda c, h: Wo[h][:, c, :],
                        C).then_inc(final_made, 1)

            turn_context(0)
            if cross:
                for job in jobs[0:KJ]:
                    make(0, 0, job, before_rows=True)
                pe.wait_ge(kept["k"], at(KJ - 1))
                turn_rows(0)
            else:
                turn_rows(0)
                for job in jobs[0:KJ]:
                    make(0, 0, job)
            for job in jobs[KJ:]:
                make(0, 0, job)
            scores(0, 0, 0)
            turn_context(1)
            if not cross:
                turn_rows(1)
            for u in range(1, LEAD):
                scores(0, 0, u)

            def body(g, par, left, first=False):
                for u in range(U):
                    turn_first = not grouped and u == U - LEAD
                    if turn_first:
                        turn_probs(g * U + u, u)
                    if left or u + LEAD < U:
                        scores(*ahead(g, par, u))
                    if not turn_first:
                        turn_probs(g * U + u, u)
                    if cross and left and u == 0:
                        turn_rows(g + 1)
                    if u == 0 and not first:
                        project_output(g * GB - 1)
                    if u == UB:
                        project_output(g * GB)
                    if left:
                        for job in before.get(u, ()):
                            make(g + 1, 1 - par, job)
                    outputs(g, par, u)
                    if left:
                        for job in after.get(u, ()):
                            make(g + 1, 1 - par, job)
                if left >= 2:
                    turn_context(g + 2)
                    if not cross:
                        turn_rows(g + 2)
                if not left:
                    project_output(g * GB + 1)

            body(0, 0, 2, first=True)
            body(1, 1, 2)
            over_groups(pe, G, body, first=2)


def mlp_phase(nc, sems, s, X, ident, minus_half, *, eps, w1, b1, w2, b2, ln_s, ln_b):
    D, C, G, M = s.D, s.C, s.G, s.M
    A_AT = M // 2
    with ExitStack() as ctx:
        def sb(n, shape, dt=F32):
            return ctx.enter_context(nc.sbuf_tensor(f"mlp_{n}", shape, dt))

        def sem(n):
            return sems.named(n)

        W1 = [sb(f"W1{h}", [P, C, s.F], F32R) for h in "hl"]
        W2 = [sb(f"W2{h}", [P, M, D], F32R) for h in "hl"]
        w2v = weight(w2)
        units = []
        for m in range(0, M, 2):
            n = slice(m * P, (m + 2) * P)
            units += [(weight(w1)[:, :, n], W1[0][:, :, n], W1[1][:, :, n]),
                      (w2v[:, m:m + 2, :], W2[0][:, m:m + 2, :], W2[1][:, m:m + 2, :])]
        stage = sb("stage", [P, 2, P * C * 2])

        weights = Weights(nc, sems, stage, units)

        xT = [sb(f"xT{h}", [P, 2, C, TOK], F32R) for h in "hl"]
        zs = sb("zs", [P, GB, D])
        affine = sb("affine", [P, GB, C, P])
        ln_cols = sb("ln_cols", [P, 2, C])
        b1_cols = sb("b1_cols", [P, M])
        row_bias = sb("row_bias", [P, D])
        stats = sb("stats", [P, GB, 6])
        tick = sb("tick", [P, 2])
        mean_var = sb("mean_var", [P, GB, 4])
        hidden = sb("hidden", [P, 4, TOK])
        hT = [sb(f"hT{h}", [P, 4, TOK], F32R) for h in "hl"]
        sums = ctx.enter_context(nc.psum_tensor("mlp_sums", [P, 2, GB, BANK], F32))
        turned = ctx.enter_context(nc.psum_tensor("mlp_turned", [P, GB, BANK], F32))
        work = ctx.enter_context(nc.psum_tensor("mlp_work", [P, 2, BANK], F32))

        small_in = sem("small_in")
        stats_done, aggr_done, eps_added, rstd_done, z_done = (
            sem(n) for n in ("stats_done", "aggr_done", "eps_added", "rstd_done", "z_done"))
        row_added, x_turned, x_affine, x_high, x_low = (
            sem(n) for n in ("row_added", "x_turned", "x_affine", "x_high", "x_low"))
        hidden_made, gelu_done, h_high, h_low, chunk_used, x_added = (
            sem(n) for n in ("hidden_made", "gelu_done", "h_high", "h_low", "chunk_used", "x_added"))
        block = ctx.enter_context(nc.Block())

        def ahead(g, par, m):
            return (g, par, m + 2) if m + 2 < M else (g + 1, 1 - par, m + 2 - M)

        @block.sync
        def _(sp):
            sp.dma_start(ln_cols[:, 0, :], column(ln_s), allow_slow_non_contiguous=True).then_inc(small_in, 16)
            sp.dma_start(ln_cols[:, 1, :], column(ln_b), allow_slow_non_contiguous=True).then_inc(small_in, 16)
            sp.dma_start(b1_cols[:, :], column(b1), allow_slow_non_contiguous=True).then_inc(small_in, 16)
            sp.dma_start(row_bias[:, :], b2.partition_broadcast(P)).then_inc(small_in, 16)
            for i in range(len(units)):
                weights.load(sp, i)

        @block.gpsimd
        def _(pool):
            for done in (rstd_done, row_added):
                pool.sem_inc(done, AHEAD)
            pool.wait_ge(small_in, 16 * 4)

            def side(g):
                pool.wait_ge(eps_added, at(g))
                nc.gpsimd.tensor_tensor(mean_var[:, :, 3], mean_var[:, :, 2], minus_half[:, 0:GB],
                                        ALU.pow).then_inc(rstd_done, 1)
                for b in range(GB):
                    pool.wait_ge(z_done, at(g * GB + b))
                    xb = X[:, bass.ds(g * GB + b, 1), :].rearrange("p b d -> p (b d)")
                    nc.gpsimd.tensor_tensor(xb, xb, row_bias[:, :], ALU.add).then_inc(row_added, 1)

            side(0)

            def body(g, par, left):
                if left:
                    side(g + 1)

            over_groups(pool, G, body)

        @block.scalar
        def _(act):
            for done in (gelu_done, x_affine):
                act.sem_inc(done, AHEAD)
            act.wait_ge(small_in, 16 * 4)

            def affine_rows(g):
                for b in range(GB):
                    act.wait_ge(x_turned, at(g * GB + b))
                    act.wait_ge(x_low, at((g - 1) * GB + b))
                    for c in range(C):
                        ins = nc.scalar.activation(affine[:, b, c, :], turned[:, b, c * P:(c + 1) * P], ACT.Identity,
                                                   bias=ln_cols[:, 1, c:c + 1], scale=ln_cols[:, 0, c:c + 1])
                    ins.then_inc(x_affine, 1)

            def gelu(g, par, m):
                n = g * M + m
                act.wait_ge(hidden_made, at(n))
                act.wait_ge(h_low, at(n - 4))
                nc.scalar.activation(hidden[:, m % 4, :], work[:, m % 2, 0:TOK], ACT.Gelu_apprx_tanh,
                                     bias=b1_cols[:, m:m + 1]).then_inc(gelu_done, 1)

            weights.round_high(act, 0)
            affine_rows(0)
            weights.round_high(act, 1)
            weights.round_high(act, 2)
            gelu(0, 0, 0)
            gelu(0, 0, 1)
            weights.round_high(act, 3)

            def body(g, par, left, first=False):
                for m in range(M):
                    if first and m + 4 < len(units):
                        weights.round_high(act, m + 4)
                    if left or m + 2 < M:
                        gelu(*ahead(g, par, m))
                    if m == A_AT and left:
                        affine_rows(g + 1)

            body(0, 0, 2, first=True)
            body(1, 1, 2)
            over_groups(act, G, body, first=2)

        @block.vector
        def _(dve):
            for done in (x_low, x_high, x_added, z_done, stats_done, aggr_done, eps_added, h_high, h_low):
                dve.sem_inc(done, AHEAD)

            def x_row(g, b):
                return X[:, bass.ds(g * GB + b, 1), :].rearrange("p b d -> p (b d)")

            def normalise(g):
                dve.wait_ge(x_turned, at(g * GB - 1))
                for b in range(GB):
                    nc.vector.bn_stats(stats[:, b, :], x_row(g, b)).then_inc(stats_done, 1)
                dve.wait_ge(stats_done, at(g * GB + GB - 1))
                nc.vector.memset(tick[:, 0:1], 0.0)
                for b in range(GB):
                    nc.vector.bn_aggr(mean_var[:, b, 0:2], stats[:, b, :]).then_inc(aggr_done, 1)
                dve.wait_ge(aggr_done, at(g * GB + GB - 1))
                nc.vector.tensor_scalar(mean_var[:, :, 2], mean_var[:, :, 1], eps, None,
                                        ALU.add).then_inc(eps_added, 1)
                dve.wait_ge(rstd_done, at(g))
                for b in range(GB):
                    nc.vector.tensor_scalar(zs[:, b, :], x_row(g, b), mean_var[:, b, 0:1], mean_var[:, b, 3:4],
                                            ALU.subtract, ALU.mult).then_inc(z_done, 1)

            def x_halves(g, par):
                dve.wait_ge(hidden_made, at((g - 1) * M - 1))
                for b in range(GB):
                    tok = slice(b * P, (b + 1) * P)
                    dve.wait_ge(x_affine, at(g * GB + b))
                    nc.vector.tensor_copy(xT[0][:, par, :, tok], affine[:, b, :, :]).then_inc(x_high, 1)
                    dve.wait_ge(x_high, at(g * GB + b))
                    nc.vector.tensor_tensor(xT[1][:, par, :, tok], affine[:, b, :, :],
                                            xT[0][:, par, :, tok].bitcast(F32), ALU.subtract).then_inc(x_low, 1)

            def hidden_halves(g, par, m):
                n = g * M + m
                dve.wait_ge(gelu_done, at(n))
                dve.wait_ge(chunk_used, at(n - 4))
                nc.vector.tensor_copy(hT[0][:, m % 4, :], hidden[:, m % 4, :]).then_inc(h_high, 1)
                dve.wait_ge(h_high, at(n))
                nc.vector.tensor_tensor(hT[1][:, m % 4, :], hidden[:, m % 4, :],
                                        hT[0][:, m % 4, :].bitcast(F32), ALU.subtract).then_inc(h_low, 1)

            normalise(0)
            weights.subtract_high(dve, 0)
            x_halves(0, 0)
            weights.subtract_high(dve, 1)
            weights.subtract_high(dve, 2)
            hidden_halves(0, 0, 0)
            hidden_halves(0, 0, 1)
            weights.subtract_high(dve, 3)

            def body(g, par, left, first=False):
                for m in range(M):
                    if first and m + 4 < len(units):
                        weights.subtract_high(dve, m + 4)
                    if left or m + 2 < M:
                        hidden_halves(*ahead(g, par, m))
                    if left and m == A_AT - 2:
                        normalise(g + 1)
                    if left and m == A_AT:
                        x_halves(g + 1, 1 - par)
                for b in range(GB):
                    dve.wait_ge(row_added, at(g * GB + b))
                    dve.wait_ge(chunk_used, at(g * M + M - 1))
                    nc.vector.tensor_tensor(x_row(g, b), sums[:, par, b, :], x_row(g, b), ALU.add).then_inc(x_added, 1)

            body(0, 0, 2, first=True)
            body(1, 1, 2)
            over_groups(dve, G, body, first=2)

        @block.tensor
        def _(pe):
            for done in (x_turned, chunk_used, hidden_made):
                pe.sem_inc(done, AHEAD)

            def turn_rows(g):
                for b in range(GB):
                    pe.wait_ge(z_done, at(g * GB + b))
                    pe.wait_ge(x_affine, at((g - 1) * GB + b))
                    for c in range(C):
                        mm = nc.tensor.transpose(turned[:, b, c * P:(c + 1) * P], zs[:, b, c * P:(c + 1) * P],
                                                 ident[:, :])
                    mm.then_inc(x_turned, 1)

            def hidden_chunk(g, par, m, first=False):
                n = g * M + m
                if first and m % 2 == 0:
                    weights.wait_split(pe, m)
                if m == 0:
                    pe.wait_ge(x_low, at(g * GB + GB - 1))
                pe.wait_ge(gelu_done, at(n - 2))
                project(nc, work[:, m % 2, 0:TOK], lambda c, h: W1[h][:, c, m * P:(m + 1) * P],
                        lambda c, h: xT[h][:, par, c, :], C).then_inc(hidden_made, 1)

            turn_rows(0)
            hidden_chunk(0, 0, 0, True)
            hidden_chunk(0, 0, 1, True)

            def body(g, par, left, first=False):
                for m in range(M):
                    n = g * M + m
                    pe.wait_ge(h_low, at(n))
                    if first and m % 2 == 0:
                        weights.wait_split(pe, m + 1)
                    if m == 0:
                        pe.wait_ge(x_added, at((g - 1) * GB - 1))
                    for b in range(GB):
                        tok = slice(b * P, (b + 1) * P)
                        for k, (ha, hb) in enumerate(((1, 0), (0, 1), (0, 0))):
                            mm = nc.tensor.matmul(sums[:, par, b, :], hT[ha][:, m % 4, tok], W2[hb][:, m, :],
                                                  start=m == 0 and k == 0, stop=m == M - 1 and k == 2)
                    mm.then_inc(chunk_used, 1)
                    if left or m + 2 < M:
                        hidden_chunk(*ahead(g, par, m), first)
                    if left and m == A_AT:
                        turn_rows(g + 1)

            body(0, 0, 2, first=True)
            body(1, 1, 2)
            over_groups(pe, G, body, first=2)


def set_up_constants(nc, sems, ident, minus_half):
    with ExitStack() as ctx:
        set_up = sems.named("set_up")
        block = ctx.enter_context(nc.Block())

        @block.gpsimd
        def _(pool):
            nc.gpsimd.memset(ident[:, :], 0.0).then_inc(set_up, 1)
            nc.gpsimd.memset(minus_half[:, :], -0.5).then_inc(set_up, 1)
            pool.wait_ge(set_up, 2)
            nc.gpsimd.affine_select(out=ident[:, :], in_=ident[:, :], compare_op=ALU.not_equal, fill=1.0, base=0,
                                    pattern=[[-1, P]], channel_multiplier=1).then_inc(set_up, 1)
            pool.wait_ge(set_up, 3)


def build_cross_attention_layers(nc, a, out):
    s = Shape(a["x"], a["L0_xattn_w1"])
    D = s.D
    with ExitStack() as ctx:
        sems = Semaphores(nc, ctx)
        X = ctx.enter_context(nc.sbuf_tensor("X", [P, s.NB, D], F32))
        ident = ctx.enter_context(nc.sbuf_tensor("ident", [P, P], F32))
        minus_half = ctx.enter_context(nc.sbuf_tensor("minus_half", [P, GB], F32))
        set_up_constants(nc, sems, ident, minus_half)
        w_qkv, b_qkv = a["L0_xattn_w_qkv"], a["L0_xattn_b_qkv"]
        attention_phase(
            nc, sems, s, "self", X, ident, minus_half, x_in=a["x"], cross=False, grouped=False, eps=1e-5, ctx_in=None,
            mask_in=a["mask_1x1xSxS2_fc1"], mask_multiplies=True, mask_per_sequence=False,
            weights=(w_qkv[:, 0:D], w_qkv[:, D:2 * D], w_qkv[:, 2 * D:3 * D], a["L0_xattn_w_ao"]),
            bias_q=b_qkv[0:D], bias_k=b_qkv[D:2 * D], bias_v=b_qkv[2 * D:3 * D], bias_o=a["L0_xattn_b_ao"],
            ln_s=a["L0_xattn_ln1_s"], ln_b=a["L0_xattn_ln1_b"], scale=32 ** -0.5, finish=None)
        sems.clear()
        w_kv, b_kv = a["L0_xattn_w_kv"], a["L0_xattn_b_kv"]
        attention_phase(
            nc, sems, s, "cross", X, ident, minus_half, cross=True, grouped=False, eps=1e-5, ctx_in=a["ctx_2048"],
            mask_in=a["mask_Bx1xSxS2_ff1"], mask_multiplies=True, mask_per_sequence=True,
            weights=(a["L0_xattn_w_q"], w_kv[:, 0:D], w_kv[:, D:2 * D], a["L0_xattn_w_co"]),
            bias_q=a["L0_xattn_b_q"], bias_k=b_kv[0:D], bias_v=b_kv[D:2 * D], bias_o=a["L0_xattn_b_co"],
            ln_s=a["L0_xattn_ln2_s"], ln_b=a["L0_xattn_ln2_b"], scale=32 ** -0.5, finish=None)
        sems.clear()
        mlp_phase(nc, sems, s, X, ident, minus_half, eps=1e-5, w1=a["L0_xattn_w1"], b1=a["L0_xattn_b1"],
                  w2=a["L0_xattn_w2"], b2=a["L0_xattn_b2"], ln_s=a["L0_xattn_ln3_s"], ln_b=a["L0_xattn_ln3_b"])
        sems.clear()
        attention_phase(
            nc, sems, s, "grouped", X, ident, minus_half, cross=True, grouped=True, eps=None, ctx_in=a["ctx_2048"],
            mask_in=a["mask_Bx1xSxS2_ff0"], mask_multiplies=False, mask_per_sequence=True,
            weights=(a["L1_xattn_Wq"], a["L1_xattn_Wk"], a["L1_xattn_Wv"], a["L1_xattn_Wo"]),
            bias_q=a["L1_xattn_bq"], bias_k=a["L1_xattn_bk"], bias_v=a["L1_xattn_bv"], bias_o=a["L1_xattn_bo"],
            ln_s=None, ln_b=None, scale=16 ** -0.5,
            finish=(a["L1_xattn_gamma"], a["L1_xattn_beta"], 1e-6, out))


def kernel(**inputs):
    import numpy as np
    import concourse.bacc as bacc
    from concourse.bass_utils import run_bass_kernel_spmd

    nc = bacc.Bacc("TRN2", target_bir_lowering=False, num_devices=1)
    arrays, args = {}, {}
    for name, value in inputs.items():
        a = np.ascontiguousarray(value)
        arrays[f"in_{name}_dram"] = a
        args[name] = nc.dram_tensor(f"in_{name}_dram", a.shape, mybir.dt.from_np(a.dtype), kind="ExternalInput").ap()
    x = arrays["in_x_dram"]
    out = nc.dram_tensor("out_dram", x.shape, mybir.dt.from_np(x.dtype), kind="ExternalOutput").ap()
    build_cross_attention_layers(nc, args, out)
    r = run_bass_kernel_spmd(nc, [arrays], core_ids=[0])
    return r.results[0]["out_dram"]
```
